# Optimizing a Trainium2 kernel written in Bass

```python
import numpy as np
import jax
import jax.numpy as jnp

def _softmax(x, axis=-1):
    return jax.nn.softmax(x, axis=axis)
def _gelu(x):
    return jax.nn.gelu(x, approximate=True)
def _silu(x):
    return jax.nn.silu(x)
def _sigmoid(x):
    return jax.nn.sigmoid(x)
def _layernorm(x, axis=-1, eps=1e-5):
    m = jnp.mean(x, axis=axis, keepdims=True)
    v = jnp.var(x, axis=axis, keepdims=True)
    return (x - m) / jnp.sqrt(v + eps)
def _scatter_add(tgt, idx, src, axis=0):
    return tgt.at[idx].add(src)
def _segment_sum(src, seg, n):
    return jax.ops.segment_sum(src, seg, n)

kernel_name = 'mk_adj_preln_d4_adj_512_51003b'

def setup_inputs(seed: int = 0):
    np.random.seed(seed)
    _w = jnp.asarray
    def _rec_inputs():
        import jax
        import jax.numpy as jnp
        _gk = jax.random.key(seed)
        x = -0.0003929 + 0.9999 * jax.random.normal(jax.random.fold_in(_gk, 1), (128, 64, 512), jnp.float32)
        _w = (1.0 + jnp.arange(64, dtype=jnp.float32)) ** -0.5
        _w = _w / _w.mean()
        _pij = jnp.clip(0.0625 * _w[:, None] * _w[None, :], 0.0, 1.0)
        _a = jax.random.uniform(jax.random.fold_in(_gk, 2), (64, 64)) < _pij
        _a = jnp.logical_or(_a, jnp.swapaxes(_a, -1, -2))
        _a = jnp.logical_or(_a, jnp.eye(64, dtype=bool))
        _af = _a.astype(jnp.float32)
        _af = _af * jax.random.uniform(jax.random.fold_in(_gk, 3), (64, 64), jnp.float32, 0.05, 1)
        adj = _af
        return x, adj
    x, adj = _rec_inputs()
    def _L0_gnn_setup():
        import jax, jax.numpy as jnp
        import numpy as np
        B, N, F_IN, F_OUT = (16, 2048, 512, 512)
        key = jax.random.key(seed)
        k1, k2, k3 = jax.random.split(key, 3)
        x = jax.random.normal(k1, (B, N, F_IN), dtype=jnp.float32)
        adj = jax.random.uniform(k2, (N, N), dtype=jnp.float32)
        bound = np.sqrt(6.0 / F_OUT)
        weight = jax.random.uniform(k3, (F_IN, F_OUT), dtype=jnp.float32, minval=-bound, maxval=bound)
        bias = jnp.zeros((F_OUT,), dtype=jnp.float32)
        return {'x': x, 'adj': adj, 'weight': weight, 'bias': bias}
    _L0_gnn_all = _L0_gnn_setup()
    _L0_gnn_in = {k: v for k, v in _L0_gnn_all.items() if k in ('weight', 'bias', )}
    del _L0_gnn_all

    def _L1_gnn_setup():
        import jax, jax.numpy as jnp
        import numpy as np
        B, N, D = (8, 2048, 512)
        key = jax.random.key(seed)
        k1, k2, k3, k4, k5 = jax.random.split(key, 5)
        neuron_states = jax.random.normal(k1, (B, N, D), dtype=jnp.float32)
        adjacency = jax.random.randint(k2, (N, N), 0, 2).astype(jnp.float32)
        scale = 1.0 / np.sqrt(D)
        Wq = jax.random.normal(k3, (D, D), dtype=jnp.float32) * scale
        Wk = jax.random.normal(k4, (D, D), dtype=jnp.float32) * scale
        Wv = jax.random.normal(k5, (D, D), dtype=jnp.float32) * scale
        return {'neuron_states': neuron_states, 'adjacency': adjacency, 'Wq': Wq, 'Wk': Wk, 'Wv': Wv}
    _L1_gnn_all = _L1_gnn_setup()
    _L1_gnn_in = {k: v for k, v in _L1_gnn_all.items() if k in ('Wq', 'Wk', 'Wv', )}
    del _L1_gnn_all

    def _L2_gnn_setup():
        import jax, jax.numpy as jnp
        import numpy as np
        B, N, D, H = (16, 1025, 512, 8)
        LN_EPS = 1e-05

        def _make_mask(key, n):
            n_proto = n - 1
            adj = jax.random.bernoulli(key, 0.03, (n_proto, n_proto)).astype(jnp.float32)
            adj = jnp.clip(adj + adj.T + jnp.eye(n_proto, dtype=jnp.float32), 0.0, 1.0)
            mask = jnp.zeros((n, n), dtype=jnp.float32)
            mask = mask.at[0, :].set(1.0).at[:, 0].set(1.0)
            mask = mask.at[1:, 1:].set(adj)
            return mask
        key = jax.random.key(seed)
        ks = jax.random.split(key, 7)
        s = 1.0 / np.sqrt(D)
        return {'x': jax.random.normal(ks[0], (B, N, D), dtype=jnp.float32), 'w_qkv': jax.random.uniform(ks[1], (D, 3 * D), dtype=jnp.float32, minval=-s, maxval=s), 'w_proj': jax.random.uniform(ks[2], (D, D), dtype=jnp.float32, minval=-s, maxval=s), 'b_proj': jnp.zeros((D,), dtype=jnp.float32), 'ln_gamma': jnp.ones((D,), dtype=jnp.float32), 'ln_beta': jnp.zeros((D,), dtype=jnp.float32), 'attn_mask': _make_mask(ks[3], N)}
    _L2_gnn_all = _L2_gnn_setup()
    _L2_gnn_in = {k: v for k, v in _L2_gnn_all.items() if k in ('w_qkv', 'w_proj', 'b_proj', 'ln_gamma', 'ln_beta', )}
    del _L2_gnn_all

    def _L3_gnn_setup():
        import jax, jax.numpy as jnp
        import numpy as np
        B, N, D = (4, 2048, 512)
        H, HD = (8, 64)
        key = jax.random.key(seed)
        ks = jax.random.split(key, 6)
        x = jax.random.normal(ks[0], (B, N, D), dtype=jnp.float32)
        adj = (jax.random.uniform(ks[1], (N, N)) < 0.1).astype(jnp.float32)
        adj = jnp.maximum(adj, jnp.eye(N, dtype=jnp.float32))
        s = 0.02
        Wq = jax.random.normal(ks[2], (D, H * HD), dtype=jnp.float32) * s
        Wk = jax.random.normal(ks[3], (D, H * HD), dtype=jnp.float32) * s
        Wv = jax.random.normal(ks[4], (D, H * HD), dtype=jnp.float32) * s
        bq = jnp.zeros((H * HD,), dtype=jnp.float32)
        bk = jnp.zeros((H * HD,), dtype=jnp.float32)
        bv = jnp.zeros((H * HD,), dtype=jnp.float32)
        return {'x': x, 'adj': adj, 'Wq': Wq, 'bq': bq, 'Wk': Wk, 'bk': bk, 'Wv': Wv, 'bv': bv}
    _L3_gnn_all = _L3_gnn_setup()
    _L3_gnn_in = {k: v for k, v in _L3_gnn_all.items() if k in ('Wq', 'bq', 'Wk', 'bk', 'Wv', 'bv', )}
    del _L3_gnn_all

    return {
        "x": x,
        "adj": adj,
        "L0_gnn_weight": _L0_gnn_in["weight"],
        "L0_gnn_bias": _L0_gnn_in["bias"],
        "L1_gnn_Wq": _L1_gnn_in["Wq"],
        "L1_gnn_Wk": _L1_gnn_in["Wk"],
        "L1_gnn_Wv": _L1_gnn_in["Wv"],
        "L2_gnn_w_qkv": _L2_gnn_in["w_qkv"],
        "L2_gnn_w_proj": _L2_gnn_in["w_proj"],
        "L2_gnn_b_proj": _L2_gnn_in["b_proj"],
        "L2_gnn_ln_gamma": _L2_gnn_in["ln_gamma"],
        "L2_gnn_ln_beta": _L2_gnn_in["ln_beta"],
        "L3_gnn_Wq": _L3_gnn_in["Wq"],
        "L3_gnn_bq": _L3_gnn_in["bq"],
        "L3_gnn_Wk": _L3_gnn_in["Wk"],
        "L3_gnn_bk": _L3_gnn_in["bk"],
        "L3_gnn_Wv": _L3_gnn_in["Wv"],
        "L3_gnn_bv": _L3_gnn_in["bv"],
    }

def reference(x, adj, L0_gnn_weight, L0_gnn_bias, L1_gnn_Wq, L1_gnn_Wk, L1_gnn_Wv, L2_gnn_w_qkv, L2_gnn_w_proj, L2_gnn_b_proj, L2_gnn_ln_gamma, L2_gnn_ln_beta, L3_gnn_Wq, L3_gnn_bq, L3_gnn_Wk, L3_gnn_bk, L3_gnn_Wv, L3_gnn_bv):
    import jax
    import jax.numpy as jnp
    def _L0_gnn_ref(x, adj, weight, bias):
        import jax, jax.numpy as jnp
        import numpy as np
        B, N, F_IN, F_OUT = (16, 2048, 512, 512)
        deg = adj.sum(axis=1)
        deg_inv_sqrt = jnp.where(deg > 0, jax.lax.rsqrt(deg), 0.0)
        norm_adj = adj * deg_inv_sqrt[:, None] * deg_inv_sqrt[None, :]
        support = jnp.einsum('bni,io->bno', x, weight)
        output = jnp.einsum('nm,bmo->bno', norm_adj, support)
        return output + bias

    def _L1_gnn_ref(neuron_states, adjacency, Wq, Wk, Wv):
        import jax, jax.numpy as jnp
        import numpy as np
        B, N, D = (8, 2048, 512)
        q = jnp.einsum('bnd,ed->bne', neuron_states, Wq)
        k = jnp.einsum('bnd,ed->bne', neuron_states, Wk)
        v = jnp.einsum('bnd,ed->bne', neuron_states, Wv)
        rel = jnp.einsum('bnd,bmd->bnm', q, k)
        rel = adjacency.T[None, :, :] * rel
        rel = rel / jnp.linalg.norm(rel, axis=2, keepdims=True)
        return jnp.einsum('bnm,bmd->bnd', rel, v)

    def _L2_gnn_ref(x, w_qkv, w_proj, b_proj, ln_gamma, ln_beta, attn_mask):
        import jax, jax.numpy as jnp
        import numpy as np
        B, N, D, H = (16, 1025, 512, 8)
        LN_EPS = 1e-05

        def _make_mask(key, n):
            n_proto = n - 1
            adj = jax.random.bernoulli(key, 0.03, (n_proto, n_proto)).astype(jnp.float32)
            adj = jnp.clip(adj + adj.T + jnp.eye(n_proto, dtype=jnp.float32), 0.0, 1.0)
            mask = jnp.zeros((n, n), dtype=jnp.float32)
            mask = mask.at[0, :].set(1.0).at[:, 0].set(1.0)
            mask = mask.at[1:, 1:].set(adj)
            return mask
        b, n, d = x.shape
        hd = d // H
        scale = hd ** (-0.5)
        qkv = (x @ w_qkv).reshape(b, n, 3, H, hd).transpose(2, 0, 3, 1, 4)
        q, k, v = (qkv[0], qkv[1], qkv[2])
        attn = jnp.einsum('bhnd,bhmd->bhnm', q, k) * scale
        attn = jnp.where(attn_mask[None, None] == 0, -jnp.inf, attn)
        attn = jax.nn.softmax(attn, axis=-1)
        o = jnp.einsum('bhnm,bhmd->bhnd', attn, v).transpose(0, 2, 1, 3).reshape(b, n, d)
        o = o @ w_proj + b_proj
        mu = jnp.mean(o, axis=-1, keepdims=True)
        var = jnp.mean(jnp.square(o - mu), axis=-1, keepdims=True)
        ln = (o - mu) * jax.lax.rsqrt(var + LN_EPS) * ln_gamma + ln_beta
        return o + ln

    def _L3_gnn_ref(x, adj, Wq, bq, Wk, bk, Wv, bv):
        import jax, jax.numpy as jnp
        import numpy as np
        B, N, D = (4, 2048, 512)
        H, HD = (8, 64)
        b, n, _ = x.shape
        q = (x @ Wq + bq).reshape(b, n, H, HD)
        k = (x @ Wk + bk).reshape(b, n, H, HD)
        v = (x @ Wv + bv).reshape(b, n, H, HD)
        scores = jnp.einsum('bihd,bjhd->bhij', q, k) / jnp.sqrt(jnp.float32(HD))
        mask = jnp.where(adj == 0, jnp.float32(-1000000000.0), jnp.float32(0.0))
        scores = scores + mask[None, None, :, :]
        weights = jax.nn.softmax(scores, axis=-1)
        out = jnp.einsum('bhij,bjhd->bihd', weights, v)
        return out.reshape(b, n, H * HD)

    h = jnp.maximum(_layernorm(x, axis=-1), 0.0)
    x = x + _L0_gnn_ref(h, adj, L0_gnn_weight, L0_gnn_bias)
    h = jnp.maximum(_layernorm(x, axis=-1), 0.0)
    x = x + _L1_gnn_ref(h, adj, L1_gnn_Wq, L1_gnn_Wk, L1_gnn_Wv)
    h = jnp.maximum(_layernorm(x, axis=-1), 0.0)
    x = x + _L2_gnn_ref(h, L2_gnn_w_qkv, L2_gnn_w_proj, L2_gnn_b_proj, L2_gnn_ln_gamma, L2_gnn_ln_beta, adj)
    h = jnp.maximum(_layernorm(x, axis=-1), 0.0)
    x = x + _L3_gnn_ref(h, adj, L3_gnn_Wq, L3_gnn_bq, L3_gnn_Wk, L3_gnn_bk, L3_gnn_Wv, L3_gnn_bv)
    return x


_drawn_inputs = setup_inputs


def setup_inputs(seed=0):
    import zlib

    import numpy as np

    out = dict(_drawn_inputs(seed))
    spreads = {'L0_gnn_bias': (0.0, 0.1),
     'L2_gnn_b_proj': (0.0, 0.1),
     'L2_gnn_ln_gamma': (1.0, 0.2),
     'L2_gnn_ln_beta': (0.0, 0.1),
     'L3_gnn_bq': (0.0, 0.8),
     'L3_gnn_bk': (0.0, 0.8),
     'L3_gnn_bv': (0.0, 0.1)}
    factors = {'L3_gnn_Wq': 8.0, 'L3_gnn_Wk': 8.0}
    for name, (base, spread) in spreads.items():
        noise = np.random.default_rng([zlib.crc32(name.encode()), seed]).standard_normal(out[name].shape)
        drawn = base * np.exp(spread * noise) if base else spread * noise
        out[name] = jnp.asarray(drawn.astype(out[name].dtype))
    for name, factor in factors.items():
        out[name] = (out[name] * factor).astype(out[name].dtype)
    return out
```

```python
from contextlib import ExitStack

import concourse.bass as bass
from concourse import mybir

F32, F16 = mybir.dt.float32, mybir.dt.float16
ALU = mybir.AluOpType
ACT = mybir.ActivationFunctionType
AX = mybir.AxisListType

P = 128
LN_EPS = 1e-5
WS = 16.0
PS = 64.0
TINY = 1e-30


def wait(eng, sem, value):
    if isinstance(value, int) and value <= 0:
        return
    eng.wait_ge(sem, value)


def wait_apart(eng, sem, value, passed):
    eng.wait_ge(sem, value)
    eng.sem_inc(passed, 1)


def gnn_kernel(nc, x, adj, w0, b0, wq1, wk1, wv1, wqkv2, wp2, bp2, gam2, bet2,
               wq3, bq3, wk3, bk3, wv3, bv3, out):
    G, N, D = x.shape
    H = 8
    HD = D // H
    NT = 4
    NC = D // P
    ROWS = NT * P
    GROUPS = G * N // ROWS
    B2 = P // N
    NJ = H // 2
    assert N == HD == 64 and D == 512 and B2 == 2 and NC == NT == 4
    SCALE = HD ** -0.5
    x_rows = x.rearrange("g n d -> (g n) d")
    y_rows = out.rearrange("g n d -> (g n) d")

    with ExitStack() as ctx:
        def sb(name, shape, dt):
            return ctx.enter_context(nc.sbuf_tensor(name, shape, dt))

        def bank(name):
            return ctx.enter_context(nc.psum_tensor(name, [P, D], F32))

        def sem(name):
            return ctx.enter_context(nc.semaphore(name))

        names = ["W0", "M1", "V1", "Q2", "K2", "V2", "P2", "Q3", "K3", "V3"]
        w_hi = {n: sb(f"{n}_hi", [P, NC, D], F16) for n in names}
        w_lo = {n: sb(f"{n}_lo", [P, NC, D], F16) for n in names}
        x_in = sb("x_in", [P, NT, D], F32)
        x_mid = sb("x_mid", [P, NT, D], F32)
        x_late = sb("x_late", [P, NT, D], F32)
        work = sb("work", [P, NT, D], F32)
        h_b = sb("h_b", [P, 2, D], F32)
        h_a = sb("h_a", [P, 2, D], F32)
        ht_b_hi, ht_b_lo = (sb(f"ht_b_{s}", [P, NC, ROWS], F16) for s in ("hi", "lo"))
        ht_a_hi, ht_a_lo = (sb(f"ht_a_{s}", [P, NC, ROWS], F16) for s in ("hi", "lo"))
        q_hi, q_lo = (sb(f"q_{s}", [P, NC, ROWS], F16) for s in ("hi", "lo"))
        qb_hi, qb_lo = q_hi, q_lo
        k_hi, k_lo = (sb(f"k_{s}", [P, NC, ROWS], F16) for s in ("hi", "lo"))
        vb_hi, vb_lo = (sb(f"vb_{s}", [P, NT, D], F16) for s in ("hi", "lo"))
        v_nat = sb("v_nat", [P, 2, 2, D], F16)
        v_bd = sb("v_bd", [P, NT, 2, B2, NJ, P], F16)
        pt_hi, pt_lo = (sb(f"pt_{s}", [P, 2, NJ, P], F16) for s in ("hi", "lo"))
        rel = sb("rel", [P, 2, P], F32)
        rel_sq = sb("rel_sq", [P, 2, P], F32)
        rel_hi, rel_lo = (sb(f"rel_{s}", [P, NT, P], F16) for s in ("hi", "lo"))
        bias0, biasp, gamma, beta, biasv = (sb(n, [P, D], F32) for n in ("bias0", "biasp", "gamma", "beta", "biasv"))
        bias_q, bias_k = sb("bias_q", [P, NC], F32), sb("bias_k", [P, NC], F32)
        ident = sb("ident", [P, P], F32)
        adj_row = sb("adj_row", [P, N], F32)
        adj_bd = sb("adj_bd", [P, P], F32)
        adj_sc = sb("adj_sc", [P, P], F32)
        adj_norm_t = sb("adj_norm_t", [P, P], F32)
        mask2, mask3 = sb("mask2", [P, N], F32), sb("mask3", [P, N], F32)
        ones = sb("ones", [P, 1], F32)
        neg_half = sb("neg_half", [P, 1], F32)
        deg = sb("deg", [P, 4], F32)
        NL = 5
        bn6 = sb("bn6", [P, NL, NT, 6], F32)
        mean_var = sb("mean_var", [P, NL, NT, 2], F32)
        var_eps = sb("var_eps", [P, NL, NT], F32)
        rstd = sb("rstd", [P, NL, NT], F32)
        nbias = sb("nbias", [P, NL, NT], F32)
        row_max = sb("row_max", [P, NT, H], F32)
        row_sum = sb("row_sum", [P, NT, H], F32)
        row_inv = sb("row_inv", [P, NT, H], F32)
        rel_ssq = sb("rel_ssq", [P, NT], F32)
        rel_rn = sb("rel_rn", [P, NT], F32)

        bank_w = [bank("bank_w0"), bank("bank_w1")]
        bank_s = [bank("bank_s0"), bank("bank_s1")]
        bank_p = [bank("bank_p0"), bank("bank_p1")]
        bank_b = [bank("bank_b0"), bank("bank_b1")]

        NB, NPJ, NW, NS = 32, 28, 24, 8
        NB_HI, NP_HI, NW_HI = 16, 24, 20
        J_ADJ, J_PROJ0, J_T1, J_M1, J_V1, J_REL, J_SSQ, J_OUT1 = (4 * i for i in range(8))
        J_Q = {2: 0, 3: 16}
        J_K = {2: 4, 3: 20}
        J_V = {2: 8, 3: 24}
        J_PR2 = 12
        HI_Q, HI_K, HI_V = {2: 0, 3: 12}, {2: 4, 3: 16}, {2: 8, 3: 20}
        J_T = {2: 0, 3: 12}
        PV_ORDER = [("pt", 0), ("pt", 1), ("pv", 0), ("pt", 2), ("pv", 1), ("pt", 3), ("pv", 2), ("pv", 3)]
        J_PT = {L: [J_T[L] + 4 + PV_ORDER.index(("pt", t)) for t in range(NT)] for L in (2, 3)}
        J_PV = {L: [J_T[L] + 4 + PV_ORDER.index(("pv", t)) for t in range(NT)] for L in (2, 3)}
        WHI_T = {2: 0, 3: 12}
        WHI_PT = {2: J_PT[2], 3: [16 + t for t in range(NT)]}
        WHI_PV2 = J_PV[2]
        J_S = {2: 0, 3: 4}

        small_in, col_in, adj_in = sem("small_in"), sem("col_in"), sem("adj_in")
        stage_in = [sem(f"stage_in{i}") for i in range(3)]
        ident_ready, const_ready, zero_ready = sem("ident_ready"), sem("const_ready"), sem("zero_ready")
        setup_v, setup_p, setup_pe = sem("setup_v"), sem("setup_p"), sem("setup_pe")
        conv_hi, conv_lo = sem("conv_hi"), sem("conv_lo")
        adjt_done = sem("adjt_done")
        x_loaded, y_stored = ([sem(f"{n}{t}") for t in range(NT)] for n in ("x_loaded", "y_stored"))
        passed_v, passed_p = sem("passed_v"), sem("passed_p")
        b_done, b_hi, b_lo = sem("b_done"), sem("b_hi"), sem("b_lo")
        p_done, p_hi, p_lo = sem("p_done"), sem("p_hi"), sem("p_lo")
        w_done, w_hi_s, w_lo_s = sem("w_done"), sem("w_hi_s"), sem("w_lo_s")
        s_done, s_read = sem("s_done"), sem("s_read")
        stats_done = [sem(f"stats_done{i}") for i in range(NL)]
        mv_ready = [sem(f"mv_ready{i}") for i in range(NL)]
        ve_ready = [sem(f"ve_ready{i}") for i in range(NL)]
        rstd_ready = [sem(f"rstd_ready{i}") for i in range(NL)]
        nbias_ready = [sem(f"nbias_ready{i}") for i in range(4)]
        h_ready = [sem(f"h_ready{i}") for i in range(4)]
        xb0_ready = sem("xb0_ready")
        sq_ready, relhi_ready, rello_ready = sem("sq_ready"), sem("relhi_ready"), sem("rello_ready")
        rn_ready = sem("rn_ready")
        vbd_ready = sem("vbd_ready")
        scores_in = {L: sem(f"scores_in{L}") for L in (2, 3)}
        max_ready = {L: sem(f"max_ready{L}") for L in (2, 3)}
        sub_ready = {L: sem(f"sub_ready{L}") for L in (2, 3)}
        exp_ready = {L: sem(f"exp_ready{L}") for L in (2, 3)}
        sum_ready = {L: sem(f"sum_ready{L}") for L in (2, 3)}
        inv_ready = {L: sem(f"inv_ready{L}") for L in (2, 3)}
        prob_ready = sem("prob_ready")
        xbeta_ready, xo_ready, og_ready, x3_ready, xb3_ready, y_ready = (
            sem(n) for n in ("xbeta_ready", "xo_ready", "og_ready", "x3_ready", "xb3_ready", "y_ready"))

        stage = [x_mid, x_late, work]
        loads = [("W0", w0, 0), ("wv", wv1, 1), ("wq", wq1, 2), ("wk", wk1, 0),
                 ("Q2", wqkv2[:, 0:D], 1), ("K2", wqkv2[:, D:2 * D], 2), ("V2", wqkv2[:, 2 * D:3 * D], 0),
                 ("P2", wp2, 1), ("Q3", wq3, 2), ("K3", wk3, 0), ("V3", wv3, 1)]
        slot_turn = {}
        for n, (name, _, slot) in enumerate(loads):
            slot_turn[name] = sum(1 for m in loads[:n + 1] if m[2] == slot)
        converted = [n for n, _, _ in loads if n[0] in "WQKVP"]

        conv_count = {n: k + 1 + (2 * NC if k else 0) for k, n in enumerate(converted)}

        block = ctx.enter_context(nc.Block())

        @block.sync
        def _(sp):
            for b in range(B2):
                sp.dma_start(adj_row[b * N:(b + 1) * N, :], adj).then_inc(adj_in, 16)

            def load_rows(g):
                for t in range(NT):
                    wait(sp, b_lo, NB * (g - 1) + J_OUT1 + t + 1)
                    sp.dma_start(x_in[:, t, :], x_rows[bass.ds(g * ROWS + t * P, P), :]).then_inc(x_loaded[t], 16)

            def store_rows(g):
                for t in range(NT):
                    wait(sp, y_ready, 4 * g + t + 1)
                    sp.dma_start(y_rows[bass.ds(g * ROWS + t * P, P), :], x_late[:, t, :]).then_inc(y_stored[t], 16)

            for n, (name, src, slot) in enumerate(loads):
                if n >= 3:
                    before = [m[0] for m in loads[:n] if m[2] == slot][-1]
                    if before in converted:
                        wait(sp, conv_lo, conv_count[before])
                    else:
                        wait(sp, setup_pe, {"wv": 1, "wq": 2, "wk": 2}[before])
                sp.dma_start(stage[slot][:, :, :], src.rearrange("(c p) n -> p c n", p=P)).then_inc(stage_in[slot], 16)
                if n == 0:
                    load_rows(0)
                    for dst, src1 in ((bias0, b0), (biasp, bp2), (gamma, gam2), (beta, bet2), (biasv, bv3)):
                        sp.dma_start(dst[:, :], src1.partition_broadcast(P)).then_inc(small_in, 16)
                    for dst, src1 in ((bias_q, bq3), (bias_k, bk3)):
                        sp.dma_start(dst[:, :], src1.rearrange("(c p) -> p c", p=P),
                                     allow_slow_non_contiguous=True).then_inc(col_in, 16)

            load_rows(1)
            with sp.Fori(2, GROUPS) as i:
                load_rows(i)
                store_rows(i - 2)
            store_rows(GROUPS - 2)
            store_rows(GROUPS - 1)
            for t in range(NT):
                sp.wait_ge(y_stored[t], 16 * GROUPS)

        @block.tensor
        def _(pe):
            def passes(dst, pairs, first=True, last=True):
                n = 0
                for lhs, rhs in pairs:
                    for a, b in ((0, 0), (0, 1), (1, 0)):
                        mm = pe.matmul(dst, lhs[a], rhs[b], start=(n == 0),
                                       stop=(n == 3 * len(pairs) - 1))
                        n += 1
                return mm

            pe.wait_ge(ident_ready, 1)
            pe.wait_ge(setup_v, 6)
            pe.transpose(bank_w[0][:, 0:P], adj_sc[:, :], ident[:, :]).then_inc(adjt_done, 1)
            pe.wait_ge(stage_in[1], 16)
            turned = [bank_p[0], bank_p[1], bank_b[0], bank_b[1]]
            for dc in range(NC):
                for ec in range(NC):
                    mm = pe.transpose(turned[dc][:, ec * P:(ec + 1) * P], x_late[:, ec, dc * P:(dc + 1) * P], ident[:, :])
            mm.then_inc(setup_pe, 1)
            pe.wait_ge(stage_in[2], 16)
            pe.wait_ge(stage_in[0], 32)
            pe.wait_ge(setup_v, 7)
            prod = [bank_w[0], bank_w[1], bank_s[0], bank_s[1]]
            for fc in range(NC):
                for ec in range(NC):
                    mm = pe.matmul(prod[fc][:, :], work[:, ec, fc * P:(fc + 1) * P], x_mid[:, ec, :],
                                   start=(ec == 0), stop=(ec == NC - 1))
            mm.then_inc(setup_pe, 1)

            def b_bank(g, j):
                wait(pe, b_lo, NB * g + j - 1)
                return bank_b[j % 2]

            def adj0(g):
                for t in range(NT):
                    dst = b_bank(g, J_ADJ + t)
                    wait(pe, h_ready[0], 4 * g + t + 1)
                    for c in range(NC):
                        mm = pe.matmul(dst[:, c * P:(c + 1) * P], h_b[:, t % 2, c * P:(c + 1) * P], adj_norm_t[:, :],
                                       start=(c == 0), stop=(c == NC - 1), skip_group_check=True)
                    mm.then_inc(b_done, 1)

            def rows_product(dst, w, ht, t):
                return passes(dst[:, :], [((ht[0][:, c, t * P:(t + 1) * P], ht[1][:, c, t * P:(t + 1) * P]),
                                           (w_hi[w][:, c, :], w_lo[w][:, c, :])) for c in range(NC)])

            def cols_product(dst, w, ht, oc):
                s = slice(oc * P, (oc + 1) * P)
                return passes(dst[:, :], [((w_hi[w][:, c, s], w_lo[w][:, c, s]),
                                           (ht[0][:, c, :], ht[1][:, c, :])) for c in range(NC)])

            HT_B, HT_A = (ht_b_hi, ht_b_lo), (ht_a_hi, ht_a_lo)

            def proj0(g):
                for t in range(NT):
                    dst = b_bank(g, J_PROJ0 + t)
                    wait(pe, b_lo, NB * g + J_ADJ + t + 1)
                    rows_product(dst, "W0", HT_B, t).then_inc(b_done, 1)

            def turn1(g):
                for t in range(NT):
                    dst = b_bank(g, J_T1 + t)
                    wait(pe, h_ready[1], 4 * g + t + 1)
                    for c in range(NC):
                        mm = pe.transpose(dst[:, c * P:(c + 1) * P], h_b[:, t % 2, c * P:(c + 1) * P], ident[:, :])
                    mm.then_inc(b_done, 1)

            def query1(g):
                for c in range(NC):
                    dst = b_bank(g, J_M1 + c)
                    if c == 0:
                        wait(pe, b_lo, NB * g + J_T1 + NT)
                    cols_product(dst, "M1", HT_B, c).then_inc(b_done, 1)

            def value1(g):
                for t in range(NT):
                    dst = b_bank(g, J_V1 + t)
                    rows_product(dst, "V1", HT_B, t).then_inc(b_done, 1)

            def relation1(g):
                for t in range(NT):
                    dst = b_bank(g, J_REL + t)
                    if t == 0:
                        wait(pe, b_lo, NB * g + J_M1 + NC)
                    s = slice(t * P, (t + 1) * P)
                    passes(dst[:, 0:P], [((ht_b_hi[:, c, s], ht_b_lo[:, c, s]), (qb_hi[:, c, s], qb_lo[:, c, s]))
                                         for c in range(NC)]).then_inc(b_done, 1)
                for t in range(NT):
                    dst = b_bank(g, J_SSQ + t)
                    wait(pe, sq_ready, 4 * g + t + 1)
                    pe.matmul(dst[:, 0:1], rel_sq[:, t % 2, :], ones[:, :], start=True, stop=True).then_inc(b_done, 1)

            def out1(g):
                for t in range(NT):
                    dst = b_bank(g, J_OUT1 + t)
                    wait(pe, rello_ready, 4 * g + t + 1)
                    passes(dst[:, :], [((rel_hi[:, t, :], rel_lo[:, t, :]),
                                        (vb_hi[:, t, :], vb_lo[:, t, :]))]).then_inc(b_done, 1)

            def w_bank(g, j):
                wait(pe, w_lo_s, NW * g + j - 1)
                return bank_w[j % 2]

            def p_bank(g, j):
                wait(pe, p_lo, NPJ * g + j - 1)
                return bank_p[j % 2]

            def turn(L, g):
                for t in range(NT):
                    dst = w_bank(g, J_T[L] + t)
                    wait(pe, h_ready[L], 4 * g + t + 1)
                    for c in range(NC):
                        mm = pe.transpose(dst[:, c * P:(c + 1) * P], h_a[:, t % 2, c * P:(c + 1) * P], ident[:, :])
                    mm.then_inc(w_done, 1)

            def query_key(L, g):
                for name, j0 in ((f"Q{L}", J_Q[L]), (f"K{L}", J_K[L])):
                    for c in range(NC):
                        dst = p_bank(g, j0 + c)
                        if name[0] == "Q" and c == 0:
                            wait(pe, w_lo_s, NW * g + J_T[L] + NT)
                        cols_product(dst, name, HT_A, c).then_inc(p_done, 1)

            def scores_value(L, g):
                def value(t):
                    dst = p_bank(g, J_V[L] + t)
                    rows_product(dst, f"V{L}", HT_A, t).then_inc(p_done, 1)

                value(0)
                for t in range(NT):
                    wait(pe, s_read, NS * g + J_S[L] + t)
                    if t == 0:
                        wait(pe, p_lo, NPJ * g + J_K[L] + NC)
                    s = slice(t * P, (t + 1) * P)
                    for j in range(NJ):
                        for r in range(2):
                            f = slice(r * HD, (r + 1) * HD)
                            dst = bank_s[r][:, j * P:(j + 1) * P]
                            for n, (a, b) in enumerate(((q_hi, k_hi), (q_hi, k_lo), (q_lo, k_hi))):
                                mm = pe.matmul(dst, a[f, j, s], b[f, j, s], start=(j == 0 and n == 0),
                                               stop=(n == 2), skip_group_check=True)
                    mm.then_inc(s_done, 1)
                    if t + 1 < NT:
                        value(t + 1)

            def attend(L, g):
                for what, t in PV_ORDER:
                    if what == "pt":
                        dst = w_bank(g, J_PT[L][t])
                        if L == 2:
                            wait(pe, prob_ready, 4 * g + t + 1)
                        else:
                            wait(pe, exp_ready[3], 4 * g + t + 1)
                        for j in range(NJ):
                            mm = pe.transpose(dst[:, j * P:(j + 1) * P], work[:, t, j * P:(j + 1) * P], ident[:, :])
                        mm.then_inc(w_done, 1)
                        continue
                    dst = w_bank(g, J_PV[L][t])
                    wait(pe, w_lo_s, NW * g + J_PT[L][t] + 1)
                    wait(pe, vbd_ready, 8 * g + (4 if L == 3 else 0) + t + 1)
                    for j in range(NJ):
                        for b in range(B2):
                            q = slice(b * N, (b + 1) * N)
                            v = [v_bd[:, t, s, b, j, :] for s in range(2)]
                            p = [pt[:, t % 2, j, q] for pt in (pt_hi, pt_lo)]
                            for n, (sv, sp_) in enumerate(((0, 0), (0, 1), (1, 0))):
                                if L == 2:
                                    mm = pe.matmul(dst[:, j * P + b * N:j * P + (b + 1) * N], v[sv], p[sp_],
                                                   start=(j == 0 and b == 0 and n == 0), stop=(n == 2),
                                                   skip_group_check=True)
                                else:
                                    mm = pe.matmul(dst[q, j * P:(j + 1) * P], p[sp_], v[sv],
                                                   start=(j == 0 and n == 0), stop=(n == 2),
                                                   skip_group_check=True)
                    mm.then_inc(w_done, 1)

            def project2(g):
                for t in range(NT):
                    dst = p_bank(g, J_PR2 + t)
                    wait(pe, w_lo_s, NW * g + J_PV[2][t] + 1)
                    rows_product(dst, "P2", HT_A, t).then_inc(p_done, 1)

            def body(gb, ga):
                if ga is not None:
                    turn(2, ga)
                    query_key(2, ga)
                    scores_value(2, ga)
                if gb is not None:
                    adj0(gb)
                    proj0(gb)
                if ga is not None:
                    attend(2, ga)
                if gb is not None:
                    turn1(gb)
                    query1(gb)
                if ga is not None:
                    project2(ga)
                if gb is not None:
                    value1(gb)
                    relation1(gb)
                if ga is not None:
                    turn(3, ga)
                    query_key(3, ga)
                    scores_value(3, ga)
                if gb is not None:
                    out1(gb)
                if ga is not None:
                    attend(3, ga)

            pe.wait_ge(conv_lo, len(converted) + 2 * NC)
            body(0, None)
            body(1, 0)
            with pe.Fori(2, GROUPS) as i:
                body(i, i - 1)
            body(None, GROUPS - 1)

        @block.scalar
        def _(act):
            def hi_weights(name):
                slot = {n: s for n, _, s in loads}[name]
                wait(act, stage_in[slot], 16 * slot_turn[name])
                act.activation(w_hi[name][:, :, :], stage[slot][:, :, :], ACT.Copy, scale=WS).then_inc(conv_hi, 1)

            hi_weights("W0")
            turned = [bank_p[0], bank_p[1], bank_b[0], bank_b[1]]
            act.wait_ge(setup_pe, 1)
            for c in range(NC):
                act.activation(w_hi["V1"][:, c, :], turned[c][:, :], ACT.Copy, scale=WS).then_inc(conv_hi, 1)
            prod = [bank_w[0], bank_w[1], bank_s[0], bank_s[1]]
            act.wait_ge(setup_pe, 2)
            for c in range(NC):
                act.activation(w_hi["M1"][:, c, :], prod[c][:, :], ACT.Copy, scale=WS).then_inc(conv_hi, 1)
            for name in converted[1:]:
                hi_weights(name)
            act.wait_ge(setup_v, 11)

            def relu(L, src, h, t, g, free_sem, free_at):
                wait(act, nbias_ready[L], 4 * g + t + 1)
                wait(act, free_sem, free_at)
                act.activation(h[:, t % 2, :], src[:, t, :], ACT.Relu, bias=nbias[:, L, t:t + 1],
                               scale=rstd[:, L, t:t + 1]).then_inc(h_ready[L], 1)

            def relu0(g, t):
                relu(0, x_in, h_b, t, g, b_done, NB * g + (J_T1 + t + 3 - NB if t < 2 else J_ADJ + t - 1))

            def relu1(g, t):
                relu(1, x_in, h_b, t, g, b_done, NB * g + (J_ADJ + t + 3 if t < 2 else J_T1 + t - 1))

            def relu2(g, t):
                relu(2, x_mid, h_a, t, g, w_done, NW * g + (J_T[3] + t + 3 - NW if t < 2 else J_T[2] + t - 1))

            def relu3(g, t):
                relu(3, x_late, h_a, t, g, w_done, NW * g + (J_T[2] + t + 3 if t < 2 else J_T[3] + t - 1))

            def tile_cols(buf, t):
                return buf[:, :, t * P:(t + 1) * P]

            def chunks(bank):
                return bank[:, :].rearrange("p (c r) -> p c r", c=NC)

            def b_read(g, j, dst, shaped=False, **kw):
                wait(act, b_done, NB * g + j + 1)
                src = bank_b[j % 2]
                act.activation(dst, chunks(src) if shaped else src[:, :], ACT.Copy, **kw).then_inc(b_hi, 1)

            def adj0_hi(g, t):
                b_read(g, J_ADJ + t, tile_cols(ht_b_hi, t), True)

            def turn1_hi(g, t):
                b_read(g, J_T1 + t, tile_cols(ht_b_hi, t), True)

            def query1_hi(g, c):
                b_read(g, J_M1 + c, qb_hi[:, c, :])

            def value1_hi(g, t):
                b_read(g, J_V1 + t, vb_hi[:, t, :])

            def relation1_hi(g, t):
                wait(act, b_lo, NB * g + J_REL + t + 1)
                act.activation(rel_hi[:, t, :], rel[:, t % 2, :], ACT.Copy).then_inc(relhi_ready, 1)
                wait(act, b_done, NB * g + J_SSQ + t - 1)
                act.activation(rel_sq[:, t % 2, :], rel[:, t % 2, :], ACT.Square).then_inc(sq_ready, 1)

            def turn_hi(L, g, t):
                wait(act, w_done, NW * g + J_T[L] + t + 1)
                act.activation(tile_cols(ht_a_hi, t), chunks(bank_w[(J_T[L] + t) % 2]), ACT.Copy).then_inc(w_hi_s, 1)

            def query_key_hi(L, g, c, key):
                j = (J_K if key else J_Q)[L] + c
                wait(act, p_done, NPJ * g + j + 1)
                dst = (k_hi if key else q_hi)[:, c, :]
                if L == 3:
                    act.activation(dst, bank_p[j % 2][:, :], ACT.Identity,
                                   bias=(bias_k if key else bias_q)[:, c:c + 1]).then_inc(p_hi, 1)
                else:
                    act.activation(dst, bank_p[j % 2][:, :], ACT.Copy).then_inc(p_hi, 1)

            def value_hi(L, g, t):
                j = J_V[L] + t
                wait(act, p_done, NPJ * g + j + 1)
                wait(act, vbd_ready, 8 * g + (4 if L == 3 else 0) + t - 1)
                act.activation(v_nat[:, t % 2, 0, :], bank_p[j % 2][:, :], ACT.Copy).then_inc(p_hi, 1)

            def exp(L, g, t):
                wait(act, sub_ready[L], 4 * g + t + 1)
                act.activation(work[:, t, :], work[:, t, :], ACT.Exp, scale=SCALE / (WS * WS)).then_inc(exp_ready[L], 1)

            def weights_hi(L, g, t):
                j = J_PT[L][t]
                wait(act, w_done, NW * g + j + 1)
                act.activation(pt_hi[:, t % 2, :, :], chunks(bank_w[j % 2]), ACT.Copy, scale=PS).then_inc(w_hi_s, 1)

            def attn2_hi(g, t):
                j = J_PV[2][t]
                wait(act, w_done, NW * g + j + 1)
                act.activation(tile_cols(ht_a_hi, t), chunks(bank_w[j % 2]), ACT.Copy, scale=1.0 / PS).then_inc(w_hi_s, 1)

            def front(L, g, relu_l):
                for t in range(NT):
                    turn_hi(L, g, t)
                    if t < 2:
                        relu_l(g, t + 2)
                for key in (False, True):
                    for c in range(NC):
                        query_key_hi(L, g, c, key)
                value_hi(L, g, 0)
                for t in range(NT):
                    if t + 1 < NT:
                        value_hi(L, g, t + 1)
                    exp(L, g, t)

            def body(gb, ga):
                if ga is not None:
                    front(2, ga, relu2)
                if gb is not None:
                    relu0(gb, 0)
                    relu0(gb, 1)
                    for t in range(NT):
                        adj0_hi(gb, t)
                        if t < 2:
                            relu0(gb, t + 2)
                    relu1(gb, 0)
                    relu1(gb, 1)
                if ga is not None:
                    for what, t in PV_ORDER:
                        weights_hi(2, ga, t) if what == "pt" else attn2_hi(ga, t)
                if gb is not None:
                    for t in range(NT):
                        turn1_hi(gb, t)
                        if t < 2:
                            relu1(gb, t + 2)
                    for c in range(NC):
                        query1_hi(gb, c)
                if ga is not None:
                    relu3(ga, 0)
                    relu3(ga, 1)
                if gb is not None:
                    for t in range(NT):
                        value1_hi(gb, t)
                    for t in range(NT):
                        relation1_hi(gb, t)
                if ga is not None:
                    front(3, ga, relu3)
                    weights_hi(3, ga, 0)
                    weights_hi(3, ga, 1)
                if gb is not None:
                    relu2(gb, 0)
                if ga is not None:
                    weights_hi(3, ga, 2)
                    weights_hi(3, ga, 3)
                if gb is not None:
                    relu2(gb, 1)

            body(0, None)
            body(1, 0)
            with act.Fori(2, GROUPS) as i:
                body(i, i - 1)
            body(None, GROUPS - 1)

        @block.vector
        def _(dve):
            dve.wait_ge(adj_in, 16 * B2)
            dve.tensor_reduce(deg[:, 0:1], adj_row[:, :], AX.X, ALU.add).then_inc(setup_v, 1)
            dve.wait_ge(const_ready, 1)
            for b in range(B2):
                dve.tensor_copy(adj_bd[b * N:(b + 1) * N, b * N:(b + 1) * N], adj_row[b * N:(b + 1) * N, :])\
                   .then_inc(setup_v, 1)
            dve.wait_ge(setup_v, 3)
            dve.tensor_scalar(deg[:, 1:2], deg[:, 0:1], TINY, None, ALU.max).then_inc(setup_v, 1)
            dve.tensor_scalar(deg[:, 2:3], deg[:, 0:1], 0.0, None, ALU.is_gt).then_inc(setup_v, 1)
            dve.wait_ge(setup_v, 5)
            dve.wait_ge(setup_p, 1)
            dve.tensor_scalar(adj_sc[:, :], adj_bd[:, :], deg[:, 3:4], deg[:, 2:3], ALU.mult, ALU.mult)\
               .then_inc(setup_v, 1)
            dve.wait_ge(adjt_done, 1)
            dve.tensor_scalar(adj_norm_t[:, :], bank_w[0][:, 0:P], deg[:, 3:4], deg[:, 2:3], ALU.mult, ALU.mult)\
               .then_inc(setup_v, 1)
            dve.tensor_scalar(mask2[:, :], adj_row[:, :], 0.0, -3e38, ALU.is_equal, ALU.mult).then_inc(setup_v, 1)
            dve.tensor_scalar(mask3[:, :], adj_row[:, :], 0.0, -1e9 / SCALE * WS * WS, ALU.is_equal, ALU.mult)\
               .then_inc(setup_v, 1)
            dve.wait_ge(col_in, 32)
            dve.tensor_scalar(bias_q[:, :], bias_q[:, :], WS, None, ALU.mult).then_inc(setup_v, 1)
            dve.tensor_scalar(bias_k[:, :], bias_k[:, :], WS, None, ALU.mult).then_inc(setup_v, 1)

            slots = {n: s for n, _, s in loads}
            turned = [bank_p[0], bank_p[1], bank_b[0], bank_b[1]]
            prod = [bank_w[0], bank_w[1], bank_s[0], bank_s[1]]

            def lo_weights(n, dst, src, hi):
                dve.wait_ge(conv_hi, n)
                dve.scalar_tensor_tensor(out=dst, in0=src, scalar=WS, in1=hi, op0=ALU.mult, op1=ALU.subtract)\
                   .then_inc(conv_lo, 1)

            def lo_flat(name):
                lo_weights(conv_count[name], w_lo[name][:, :, :], stage[slots[name]][:, :, :], w_hi[name][:, :, :])

            lo_flat("W0")
            for c in range(NC):
                lo_weights(2 + c, w_lo["V1"][:, c, :], turned[c][:, :], w_hi["V1"][:, c, :])
            for c in range(NC):
                lo_weights(2 + NC + c, w_lo["M1"][:, c, :], prod[c][:, :], w_hi["M1"][:, c, :])
            for name in converted[1:]:
                lo_flat(name)
            dve.wait_ge(setup_v, 11)
            dve.wait_ge(small_in, 16 * 5)

            def stats(L, src, g, t):
                dve.bn_stats(bn6[:, L, t, :], src[:, t, :]).then_inc(stats_done[L], 1)
                wait_apart(dve, stats_done[L], 4 * g + t + 1, passed_v)
                dve.bn_aggr(mean_var[:, L, t, :], bn6[:, L, t, :]).then_inc(mv_ready[L], 1)

            def tile_cols(buf, t):
                return buf[:, :, t * P:(t + 1) * P]

            def chunks(bank):
                return bank[:, :].rearrange("p (c r) -> p c r", c=NC)

            def lo(dst, src, hi, sem_, scale=None):
                if scale is None:
                    dve.tensor_tensor(dst, src, hi, ALU.subtract).then_inc(sem_, 1)
                else:
                    dve.scalar_tensor_tensor(out=dst, in0=src, scalar=scale, in1=hi, op0=ALU.mult,
                                             op1=ALU.subtract).then_inc(sem_, 1)

            def norm0(g, t):
                wait(dve, x_loaded[t], 16 * g + 16)
                stats(0, x_in, g, t)

            def adj0_lo(g, t):
                wait(dve, b_hi, NB_HI * g + t + 1)
                lo(tile_cols(ht_b_lo, t), chunks(bank_b[(J_ADJ + t) % 2]), tile_cols(ht_b_hi, t), b_lo)

            def residual0(g, t):
                wait(dve, b_done, NB * g + J_PROJ0 + t + 1)
                wait(dve, xb0_ready, 4 * g + t + 1)
                dve.scalar_tensor_tensor(out=x_in[:, t, :], in0=bank_b[(J_PROJ0 + t) % 2][:, :], scalar=1.0 / WS,
                                         in1=x_in[:, t, :], op0=ALU.mult, op1=ALU.add).then_inc(b_lo, 1)
                wait(dve, b_lo, NB * g + J_PROJ0 + t + 1)
                stats(1, x_in, g, t)

            def turn1_lo(g, t):
                wait(dve, b_hi, NB_HI * g + 4 + t + 1)
                lo(tile_cols(ht_b_lo, t), chunks(bank_b[(J_T1 + t) % 2]), tile_cols(ht_b_hi, t), b_lo)

            def query1_lo(g, c):
                wait(dve, b_hi, NB_HI * g + 8 + c + 1)
                lo(qb_lo[:, c, :], bank_b[(J_M1 + c) % 2][:, :], qb_hi[:, c, :], b_lo)

            def value1_lo(g, t):
                wait(dve, b_hi, NB_HI * g + 12 + t + 1)
                lo(vb_lo[:, t, :], bank_b[(J_V1 + t) % 2][:, :], vb_hi[:, t, :], b_lo)

            def relation1(g, t):
                wait(dve, b_done, NB * g + J_REL + t + 1)
                wait(dve, sq_ready, 4 * g + t - 1)
                dve.scalar_tensor_tensor(out=rel[:, t % 2, :], in0=bank_b[(J_REL + t) % 2][:, 0:P],
                                         scalar=1.0 / (WS * WS), in1=adj_bd[:, :], op0=ALU.mult, op1=ALU.mult)\
                   .then_inc(b_lo, 1)

            def relation1_lo(g, t):
                wait(dve, relhi_ready, 4 * g + t + 1)
                dve.tensor_tensor(rel_lo[:, t, :], rel[:, t % 2, :], rel_hi[:, t, :], ALU.subtract)\
                   .then_inc(rello_ready, 1)

            def ssq1(g, t):
                wait(dve, b_done, NB * g + J_SSQ + t + 1)
                dve.tensor_scalar(rel_ssq[:, t:t + 1], bank_b[(J_SSQ + t) % 2][:, 0:1], WS * WS, None, ALU.mult)\
                   .then_inc(b_lo, 1)

            def residual1(g, t):
                wait(dve, b_done, NB * g + J_OUT1 + t + 1)
                wait(dve, rn_ready, 4 * g + t + 1)
                wait(dve, xo_ready, 4 * g - 3 + t)
                dve.scalar_tensor_tensor(out=x_mid[:, t, :], in0=bank_b[(J_OUT1 + t) % 2][:, :],
                                         scalar=rel_rn[:, t:t + 1], in1=x_in[:, t, :], op0=ALU.mult, op1=ALU.add)\
                   .then_inc(b_lo, 1)
                wait(dve, b_lo, NB * g + J_OUT1 + t + 1)
                stats(2, x_mid, g, t)

            def turn_lo(L, g, t):
                wait(dve, w_hi_s, NW_HI * g + WHI_T[L] + t + 1)
                lo(tile_cols(ht_a_lo, t), chunks(bank_w[(J_T[L] + t) % 2]), tile_cols(ht_a_hi, t), w_lo_s)

            def query_key_lo(L, g, c, key):
                j = (J_K if key else J_Q)[L] + c
                wait(dve, p_hi, NP_HI * g + (HI_K if key else HI_Q)[L] + c + 1)
                dst, hi = ((k_lo, k_hi) if key else (q_lo, q_hi))
                if L == 3:
                    dve.scalar_tensor_tensor(out=dst[:, c, :], in0=bank_p[j % 2][:, :],
                                             scalar=(bias_k if key else bias_q)[:, c:c + 1], in1=hi[:, c, :],
                                             op0=ALU.add, op1=ALU.subtract).then_inc(p_lo, 1)
                else:
                    lo(dst[:, c, :], bank_p[j % 2][:, :], hi[:, c, :], p_lo)

            def value_lo(L, g, t):
                j = J_V[L] + t
                wait(dve, p_hi, NP_HI * g + HI_V[L] + t + 1)
                lo(v_nat[:, t % 2, 1, :], bank_p[j % 2][:, :], v_nat[:, t % 2, 0, :], p_lo)
                wait(dve, p_lo, NPJ * g + j + 1)
                for b in range(B2):
                    for r in range(2):
                        rows = slice(r * N, (r + 1) * N)
                        src = v_nat[b * N:(b + 1) * N, t % 2, :, :].rearrange("p s (j r d) -> p s j r d", j=NJ, r=2)
                        cp = dve.tensor_copy(v_bd[rows, t, :, b, :, r * HD:(r + 1) * HD], src[:, :, :, r, :])
                cp.then_inc(vbd_ready, 1)

            def per_head(buf, t):
                return buf[:, t, :].rearrange("p (h k) -> p h k", h=H)

            def scores(L, g, t):
                mask = mask2 if L == 2 else mask3
                wait(dve, s_done, NS * g + J_S[L] + t + 1)
                for r in range(2):
                    for b in range(B2):
                        q = slice(b * N, (b + 1) * N)
                        dst = work[q, t, :].rearrange("p (j r k) -> p j r k", j=NJ, r=2)[:, :, r, :]
                        src = bank_s[r][q, :].rearrange("p (j k) -> p j k", j=NJ)[:, :, q]
                        tt = dve.tensor_tensor(dst, src, mask[q, :].unsqueeze(1).broadcast_to((N, NJ, N)), ALU.add)
                tt.then_inc(s_read, 1)

            def softmax_shift(L, g, t):
                wait(dve, s_read, NS * g + J_S[L] + t + 1)
                dve.tensor_reduce(row_max[:, t, :], per_head(work, t), AX.X, ALU.max).then_inc(max_ready[L], 1)
                wait(dve, max_ready[L], 4 * g + t + 1)
                dve.tensor_tensor(per_head(work, t), per_head(work, t),
                                  row_max[:, t, :].unsqueeze(2).broadcast_to((P, H, N)), ALU.subtract)\
                   .then_inc(sub_ready[L], 1)

            def softmax_sum(L, g, t):
                wait(dve, exp_ready[L], 4 * g + t + 1)
                dve.tensor_reduce(row_sum[:, t, :], per_head(work, t), AX.X, ALU.add).then_inc(sum_ready[L], 1)
                wait(dve, sum_ready[L], 4 * g + t + 1)
                dve.reciprocal(row_inv[:, t, :], row_sum[:, t, :]).then_inc(inv_ready[L], 1)

            def weights_lo(L, g, t):
                j = J_PT[L][t]
                wait(dve, w_hi_s, NW_HI * g + WHI_PT[L][t] + 1)
                lo(pt_lo[:, t % 2, :, :], chunks(bank_w[j % 2]), pt_hi[:, t % 2, :, :], w_lo_s, PS)

            def attn2_lo(g, t):
                j = J_PV[2][t]
                wait(dve, w_hi_s, NW_HI * g + WHI_PV2[t] + 1)
                lo(tile_cols(ht_a_lo, t), chunks(bank_w[j % 2]), tile_cols(ht_a_hi, t), w_lo_s, 1.0 / PS)

            def project2(g, t):
                j = J_PR2 + t
                wait(dve, p_done, NPJ * g + j + 1)
                dve.scalar_tensor_tensor(out=work[:, t, :], in0=bank_p[j % 2][:, :], scalar=1.0 / (WS * WS),
                                         in1=biasp[:, :], op0=ALU.mult, op1=ALU.add).then_inc(p_lo, 1)
                wait(dve, p_lo, NPJ * g + j + 1)
                stats(4, work, g, t)

            def residual2(g, t):
                wait(dve, xo_ready, 4 * g + t + 1)
                wait(dve, mv_ready[4], 4 * g + t + 1)
                dve.scalar_tensor_tensor(out=work[:, t, :], in0=work[:, t, :], scalar=mean_var[:, 4, t, 0:1],
                                         in1=gamma[:, :], op0=ALU.subtract, op1=ALU.mult).then_inc(og_ready, 1)
                wait(dve, og_ready, 4 * g + t + 1)
                wait(dve, rstd_ready[4], 4 * g + t + 1)
                dve.scalar_tensor_tensor(out=x_late[:, t, :], in0=work[:, t, :], scalar=rstd[:, 4, t:t + 1],
                                         in1=x_late[:, t, :], op0=ALU.mult, op1=ALU.add).then_inc(x3_ready, 1)
                wait(dve, x3_ready, 4 * g + t + 1)
                stats(3, x_late, g, t)

            def result(g, t):
                j = J_PV[3][t]
                wait(dve, w_done, NW * g + j + 1)
                wait(dve, inv_ready[3], 4 * g + t + 1)
                dve.tensor_tensor(per_head(work, t), bank_w[j % 2][:, :].rearrange("p (h k) -> p h k", h=H),
                                  row_inv[:, t, :].unsqueeze(2).broadcast_to((P, H, HD)), ALU.mult).then_inc(w_lo_s, 1)
                wait(dve, w_lo_s, NW * g + j + 1)
                wait(dve, xb3_ready, 4 * g + t + 1)
                dve.scalar_tensor_tensor(out=x_late[:, t, :], in0=work[:, t, :], scalar=1.0 / (WS * PS),
                                         in1=x_late[:, t, :], op0=ALU.mult, op1=ALU.add).then_inc(y_ready, 1)

            def front(L, ga, gb):
                for t in range(NT):
                    turn_lo(L, ga, t)
                for c in range(NC):
                    query_key_lo(L, ga, c, False)
                    if L == 2 and gb is not None:
                        norm0(gb, c)
                for c in range(NC):
                    query_key_lo(L, ga, c, True)
                value_lo(L, ga, 0)
                for t in range(NT):
                    scores(L, ga, t)
                    if t + 1 < NT:
                        value_lo(L, ga, t + 1)
                    softmax_shift(L, ga, t)
                for t in range(NT):
                    softmax_sum(L, ga, t)

            def body(gb, ga):
                if ga is not None:
                    front(2, ga, gb)
                elif gb is not None:
                    for t in range(NT):
                        norm0(gb, t)
                if gb is not None:
                    for t in range(NT):
                        adj0_lo(gb, t)
                    for t in range(NT):
                        residual0(gb, t)
                if ga is not None:
                    for what, t in PV_ORDER:
                        weights_lo(2, ga, t) if what == "pt" else attn2_lo(ga, t)
                if gb is not None:
                    for t in range(NT):
                        turn1_lo(gb, t)
                    for c in range(NC):
                        query1_lo(gb, c)
                if ga is not None:
                    for t in range(NT):
                        project2(ga, t)
                        if t:
                            residual2(ga, t - 1)
                    residual2(ga, NT - 1)
                if gb is not None:
                    for t in range(NT):
                        value1_lo(gb, t)
                    for t in range(NT):
                        relation1(gb, t)
                        relation1_lo(gb, t)
                    for t in range(NT):
                        ssq1(gb, t)
                if ga is not None:
                    front(3, ga, None)
                if gb is not None:
                    for t in range(NT):
                        residual1(gb, t)
                if ga is not None:
                    for what, t in PV_ORDER:
                        weights_lo(3, ga, t) if what == "pt" else result(ga, t)

            body(0, None)
            body(1, 0)
            with dve.Fori(2, GROUPS) as i:
                body(i, i - 1)
            body(None, GROUPS - 1)

        @block.gpsimd
        def _(pool):
            pool.memset(ident[:, :], 0.0).then_inc(zero_ready, 1)
            pool.memset(adj_bd[:, :], 0.0).then_inc(const_ready, 1)
            pool.memset(neg_half[:, :], -0.5).then_inc(zero_ready, 1)
            pool.memset(ones[:, :], 1.0).then_inc(zero_ready, 1)
            pool.memset(v_bd[:, :, :, :, :, :], 0.0).then_inc(zero_ready, 1)
            pool.wait_ge(zero_ready, 4)
            pool.affine_select(out=ident[:, :], in_=ident[:, :], compare_op=ALU.not_equal, fill=1.0, base=0,
                               pattern=[[-1, P]], channel_multiplier=1).then_inc(ident_ready, 1)
            pool.wait_ge(setup_v, 4)
            pool.tensor_tensor(deg[:, 3:4], deg[:, 1:2], neg_half[:, :], ALU.pow).then_inc(setup_p, 1)
            pool.wait_ge(small_in, 16 * 5)

            def root(L, g, t, bias=True):
                wait_apart(pool, mv_ready[L], 4 * g + t + 1, passed_p)
                pool.tensor_scalar(var_eps[:, L, t:t + 1], mean_var[:, L, t, 1:2], LN_EPS, None, ALU.add)\
                    .then_inc(ve_ready[L], 1)
                wait(pool, ve_ready[L], 4 * g + t + 1)
                pool.tensor_tensor(rstd[:, L, t:t + 1], var_eps[:, L, t:t + 1], neg_half[:, :], ALU.pow)\
                    .then_inc(rstd_ready[L], 1)
                if bias:
                    wait_apart(pool, rstd_ready[L], 4 * g + t + 1, passed_p)
                    pool.tensor_scalar(nbias[:, L, t:t + 1], rstd[:, L, t:t + 1], mean_var[:, L, t, 0:1], -1.0,
                                       ALU.mult, ALU.mult).then_inc(nbias_ready[L], 1)

            def add_rows(dst, a, b, sem_):
                pool.tensor_tensor(dst, a, b, ALU.add).then_inc(sem_, 1)

            def body(gb, ga):
                if gb is not None:
                    for t in range(NT):
                        root(0, gb, t)
                if ga is not None:
                    for t in range(NT):
                        wait(pool, inv_ready[2], 4 * ga + t + 1)
                        heads = work[:, t, :].rearrange("p (h k) -> p h k", h=H)
                        pool.tensor_tensor(heads, heads, row_inv[:, t, :].unsqueeze(2).broadcast_to((P, H, N)),
                                           ALU.mult).then_inc(prob_ready, 1)
                if gb is not None:
                    for t in range(NT):
                        wait(pool, h_ready[0], 4 * gb + t + 1)
                        add_rows(x_in[:, t, :], x_in[:, t, :], bias0[:, :], xb0_ready)
                    for t in range(NT):
                        root(1, gb, t)
                if ga is not None:
                    for t in range(NT):
                        wait(pool, b_lo, NB * ga + J_OUT1 + t + 1)
                        wait(pool, y_stored[t], 16 * ga)
                        add_rows(x_late[:, t, :], x_mid[:, t, :], beta[:, :], xbeta_ready)
                    for t in range(NT):
                        wait(pool, p_lo, NPJ * ga + J_PR2 + t + 1)
                        wait(pool, xbeta_ready, 4 * ga + t + 1)
                        add_rows(x_late[:, t, :], x_late[:, t, :], work[:, t, :], xo_ready)
                        root(4, ga, t, bias=False)
                        if t:
                            root(3, ga, t - 1)
                    root(3, ga, NT - 1)
                if gb is not None:
                    for t in range(NT):
                        wait(pool, b_lo, NB * gb + J_SSQ + t + 1)
                        pool.tensor_tensor(rel_rn[:, t:t + 1], rel_ssq[:, t:t + 1], neg_half[:, :], ALU.pow)\
                            .then_inc(rn_ready, 1)
                if ga is not None:
                    for t in range(NT):
                        wait(pool, h_ready[3], 4 * ga + t + 1)
                        add_rows(x_late[:, t, :], x_late[:, t, :], biasv[:, :], xb3_ready)
                if gb is not None:
                    for t in range(NT):
                        root(2, gb, t)

            body(0, None)
            body(1, 0)
            with pool.Fori(2, GROUPS) as i:
                body(i, i - 1)
            body(None, GROUPS - 1)


_INS = ['x', 'adj', 'L0_gnn_weight', 'L0_gnn_bias', 'L1_gnn_Wq', 'L1_gnn_Wk', 'L1_gnn_Wv', 'L2_gnn_w_qkv',
        'L2_gnn_w_proj', 'L2_gnn_b_proj', 'L2_gnn_ln_gamma', 'L2_gnn_ln_beta', 'L3_gnn_Wq', 'L3_gnn_bq',
        'L3_gnn_Wk', 'L3_gnn_bk', 'L3_gnn_Wv', 'L3_gnn_bv']
_OUTS = [((128, 64, 512), 'float32')]


def kernel(**inputs):
    import numpy as _np
    import concourse.bacc as _bacc
    from concourse import mybir as _mybir
    from concourse.bass_utils import run_bass_kernel_spmd as _run

    nc = _bacc.Bacc("TRN2", target_bir_lowering=False, num_devices=1)
    arrays, args = {}, []
    for name in _INS:
        a = _np.ascontiguousarray(inputs[name])
        arrays[f"in_{name}_dram"] = a
        args.append(nc.dram_tensor(f"in_{name}_dram", a.shape, _mybir.dt.from_np(a.dtype), kind="ExternalInput").ap())
    for i, (shape, dtype) in enumerate(_OUTS):
        dt = _mybir.dt.from_np(_np.dtype(dtype))
        args.append(nc.dram_tensor(f"out_{i}_dram", shape, dt, kind="ExternalOutput").ap())
    gnn_kernel(nc, *args)
    r = _run(nc, [arrays], core_ids=[0])
    got = tuple(r.results[0][f"out_{i}_dram"] for i in range(len(_OUTS)))
    return got[0]
```

```python
from contextlib import ExitStack

import concourse.bass as bass
from concourse import mybir

F32, F16 = mybir.dt.float32, mybir.dt.float16
ALU = mybir.AluOpType
ACT = mybir.ActivationFunctionType
AX = mybir.AxisListType

P = 128
LN_EPS = 1e-5
WS = 16.0
PS = 64.0
TINY = 1e-30


def wait(eng, sem, value):
    if isinstance(value, int) and value <= 0:
        return
    eng.wait_ge(sem, value)


def wait_apart(eng, sem, value, passed):
    eng.wait_ge(sem, value)
    eng.sem_inc(passed, 1)


def gnn_kernel(nc, x, adj, w0, b0, wq1, wk1, wv1, wqkv2, wp2, bp2, gam2, bet2,
               wq3, bq3, wk3, bk3, wv3, bv3, out):
    G, N, D = x.shape
    H = 8
    HD = D // H
    NT = 4
    NC = D // P
    ROWS = NT * P
    GROUPS = G * N // ROWS
    B2 = P // N
    NJ = H // 2
    assert N == HD == 64 and D == 512 and B2 == 2 and NC == NT == 4
    SCALE = HD ** -0.5
    x_rows = x.rearrange("g n d -> (g n) d")
    y_rows = out.rearrange("g n d -> (g n) d")

    with ExitStack() as ctx:
        def sb(name, shape, dt):
            return ctx.enter_context(nc.sbuf_tensor(name, shape, dt))

        def bank(name):
            return ctx.enter_context(nc.psum_tensor(name, [P, D], F32))

        def sem(name):
            return ctx.enter_context(nc.semaphore(name))

        names = ["W0", "M1", "V1", "Q2", "K2", "V2", "P2", "Q3", "K3", "V3"]
        w_hi = {n: sb(f"{n}_hi", [P, NC, D], F16) for n in names}
        w_lo = {n: sb(f"{n}_lo", [P, NC, D], F16) for n in names}
        x_in = sb("x_in", [P, NT, D], F32)
        x_mid = sb("x_mid", [P, NT, D], F32)
        x_late = sb("x_late", [P, NT, D], F32)
        work = sb("work", [P, NT, D], F32)
        h_b = sb("h_b", [P, 2, D], F32)
        h_a = sb("h_a", [P, 2, D], F32)
        ht_b_hi, ht_b_lo = (sb(f"ht_b_{s}", [P, NC, ROWS], F16) for s in ("hi", "lo"))
        ht_a_hi, ht_a_lo = (sb(f"ht_a_{s}", [P, NC, ROWS], F16) for s in ("hi", "lo"))
        q_hi, q_lo = (sb(f"q_{s}", [P, NC, ROWS], F16) for s in ("hi", "lo"))
        qb_hi, qb_lo = q_hi, q_lo
        k_hi, k_lo = (sb(f"k_{s}", [P, NC, ROWS], F16) for s in ("hi", "lo"))
        vb_hi, vb_lo = (sb(f"vb_{s}", [P, NT, D], F16) for s in ("hi", "lo"))
        v_nat = sb("v_nat", [P, 2, 2, D], F16)
        v_bd = sb("v_bd", [P, NT, 2, B2, NJ, P], F16)
        pt_hi, pt_lo = (sb(f"pt_{s}", [P, 2, NJ, P], F16) for s in ("hi", "lo"))
        rel = sb("rel", [P, NT, P], F32)
        rel_sq = sb("rel_sq", [P, NT, P], F32)
        rel_hi, rel_lo = (sb(f"rel_{s}", [P, NT, P], F16) for s in ("hi", "lo"))
        bias0, biasp, gamma, beta, biasv = (sb(n, [P, D], F32) for n in ("bias0", "biasp", "gamma", "beta", "biasv"))
        bias_q, bias_k = sb("bias_q", [P, NC], F32), sb("bias_k", [P, NC], F32)
        ident = sb("ident", [P, P], F32)
        adj_row = sb("adj_row", [P, N], F32)
        adj_bd = sb("adj_bd", [P, P], F32)
        adj_sc = sb("adj_sc", [P, P], F32)
        adj_norm_t = sb("adj_norm_t", [P, P], F32)
        mask2, mask3 = sb("mask2", [P, N], F32), sb("mask3", [P, N], F32)
        ones = sb("ones", [P, 1], F32)
        neg_half = sb("neg_half", [P, 1], F32)
        deg = sb("deg", [P, 4], F32)
        NL = 5
        bn6 = sb("bn6", [P, NL, NT, 6], F32)
        mean_var = sb("mean_var", [P, NL, NT, 2], F32)
        var_eps = sb("var_eps", [P, NL, NT], F32)
        rstd = sb("rstd", [P, NL, NT], F32)
        nbias = sb("nbias", [P, NL, NT], F32)
        row_max = sb("row_max", [P, NT, H], F32)
        row_sum = sb("row_sum", [P, NT, H], F32)
        row_inv = sb("row_inv", [P, NT, H], F32)
        rel_ssq = sb("rel_ssq", [P, NT], F32)
        rel_rn = sb("rel_rn", [P, NT], F32)

        bank_w = [bank("bank_w0"), bank("bank_w1")]
        bank_s = [bank("bank_s0"), bank("bank_s1")]
        bank_p = [bank("bank_p0"), bank("bank_p1")]
        bank_b = [bank("bank_b0"), bank("bank_b1")]

        NB, NPJ, NW, NS = 28, 28, 24, 8
        NR = 2
        NB_HI, NP_HI, NW_HI = 16, 24, 20
        J_ADJ, J_PROJ0, J_T1, J_M1 = 0, 4, 8, 12
        J_REL, J_SSQ, J_V1, J_OUT1 = 16, 19, (18, 21, 22, 23), 24
        J_Q = {2: 0, 3: 16}
        J_K = {2: 4, 3: 20}
        J_V = {2: 8, 3: 24}
        J_PR2 = 12
        HI_Q, HI_K, HI_V = {2: 0, 3: 12}, {2: 4, 3: 16}, {2: 8, 3: 20}
        PV_ORDER = [("pt", 0), ("pt", 1), ("pv", 0), ("pt", 2), ("pv", 1), ("pt", 3), ("pv", 2), ("pv", 3)]
        J_PT, J_PV = ([PV_ORDER.index((what, t)) for t in range(NT)] for what in ("pt", "pv"))
        J_S = {2: 0, 3: 4}

        def is_group(g, number):
            return isinstance(g, int) and g == number

        def w_turned(L, g):
            if L == 3:
                return NW * g + 12
            return 0 if is_group(g, 0) else NW * g - 8

        def w_attended(L, g):
            return NW * g + (4 if L == 2 else 16 if is_group(g, GROUPS - 1) else 20)

        def w_turned_hi(L, g):
            if L == 3:
                return NW_HI * g + 12
            return 0 if is_group(g, 0) else NW_HI * g - 4

        def w_attended_hi(L, g):
            return NW_HI * g + (4 if L == 2 else 16 if is_group(g, GROUPS - 1) else 20)

        small_in, col_in, adj_in = sem("small_in"), sem("col_in"), sem("adj_in")
        stage_in = [sem(f"stage_in{i}") for i in range(3)]
        ident_ready, const_ready, zero_ready = sem("ident_ready"), sem("const_ready"), sem("zero_ready")
        setup_v, setup_p, setup_pe = sem("setup_v"), sem("setup_p"), sem("setup_pe")
        conv_hi, conv_lo = sem("conv_hi"), sem("conv_lo")
        adjt_done = sem("adjt_done")
        x_loaded, y_stored = ([sem(f"{n}{t}") for t in range(NT)] for n in ("x_loaded", "y_stored"))
        passed_v, passed_p = sem("passed_v"), sem("passed_p")
        b_done, b_hi, b_lo = sem("b_done"), sem("b_hi"), sem("b_lo")
        p_done, p_hi, p_lo = sem("p_done"), sem("p_hi"), sem("p_lo")
        w_done, w_hi_s, w_lo_s = sem("w_done"), sem("w_hi_s"), sem("w_lo_s")
        s_done, s_read = sem("s_done"), sem("s_read")
        stats_done = [sem(f"stats_done{i}") for i in range(NL)]
        mv_ready = [sem(f"mv_ready{i}") for i in range(NL)]
        ve_ready = [sem(f"ve_ready{i}") for i in range(NL)]
        rstd_ready = [sem(f"rstd_ready{i}") for i in range(NL)]
        nbias_ready = [sem(f"nbias_ready{i}") for i in range(4)]
        h_ready = [sem(f"h_ready{i}") for i in range(4)]
        xb0_ready = sem("xb0_ready")
        sq_ready, relhi_ready, rello_ready = sem("sq_ready"), sem("relhi_ready"), sem("rello_ready")
        rn_ready = sem("rn_ready")
        vbd_ready, vbd_act_ready = sem("vbd_ready"), sem("vbd_act_ready")
        scores_in = {L: sem(f"scores_in{L}") for L in (2, 3)}
        max_ready = {L: sem(f"max_ready{L}") for L in (2, 3)}
        sub_ready = {L: sem(f"sub_ready{L}") for L in (2, 3)}
        exp_ready = {L: sem(f"exp_ready{L}") for L in (2, 3)}
        sum_ready = {L: sem(f"sum_ready{L}") for L in (2, 3)}
        inv_ready = {L: sem(f"inv_ready{L}") for L in (2, 3)}
        prob_ready = sem("prob_ready")
        xbeta_ready, xo_ready, og_ready, x3_ready, xb3_ready, y_ready = (
            sem(n) for n in ("xbeta_ready", "xo_ready", "og_ready", "x3_ready", "xb3_ready", "y_ready"))

        stage = [x_mid, x_late, work]
        loads = [("W0", w0, 0), ("wv", wv1, 1), ("wq", wq1, 2), ("wk", wk1, 0),
                 ("Q2", wqkv2[:, 0:D], 1), ("K2", wqkv2[:, D:2 * D], 2), ("V2", wqkv2[:, 2 * D:3 * D], 0),
                 ("P2", wp2, 1), ("Q3", wq3, 2), ("K3", wk3, 0), ("V3", wv3, 1)]
        slot_turn = {}
        for n, (name, _, slot) in enumerate(loads):
            slot_turn[name] = sum(1 for m in loads[:n + 1] if m[2] == slot)
        converted = [n for n, _, _ in loads if n[0] in "WQKVP"]

        conv_count = {n: k + 1 + (2 * NC if k else 0) for k, n in enumerate(converted)}

        block = ctx.enter_context(nc.Block())

        @block.sync
        def _(sp):
            for b in range(B2):
                sp.dma_start(adj_row[b * N:(b + 1) * N, :], adj).then_inc(adj_in, 16)

            def load_rows(g):
                for t in range(NT):
                    wait(sp, b_lo, NB * (g - 1) + J_OUT1 + t + 1)
                    sp.dma_start(x_in[:, t, :], x_rows[bass.ds(g * ROWS + t * P, P), :]).then_inc(x_loaded[t], 16)

            def store_rows(g):
                for t in range(NT):
                    wait(sp, y_ready, 4 * g + t + 1)
                    sp.dma_start(y_rows[bass.ds(g * ROWS + t * P, P), :], x_late[:, t, :]).then_inc(y_stored[t], 16)

            for n, (name, src, slot) in enumerate(loads):
                if n >= 3:
                    before = [m[0] for m in loads[:n] if m[2] == slot][-1]
                    if before in converted:
                        wait(sp, conv_lo, conv_count[before])
                    else:
                        wait(sp, setup_pe, {"wv": 1, "wq": 2, "wk": 2}[before])
                sp.dma_start(stage[slot][:, :, :], src.rearrange("(c p) n -> p c n", p=P)).then_inc(stage_in[slot], 16)
                if n == 0:
                    load_rows(0)
                    for dst, src1 in ((bias0, b0), (biasp, bp2), (gamma, gam2), (beta, bet2), (biasv, bv3)):
                        sp.dma_start(dst[:, :], src1.partition_broadcast(P)).then_inc(small_in, 16)
                    for dst, src1 in ((bias_q, bq3), (bias_k, bk3)):
                        sp.dma_start(dst[:, :], src1.rearrange("(c p) -> p c", p=P),
                                     allow_slow_non_contiguous=True).then_inc(col_in, 16)

            load_rows(1)
            with sp.Fori(2, GROUPS) as i:
                load_rows(i)
                store_rows(i - 2)
            store_rows(GROUPS - 2)
            store_rows(GROUPS - 1)
            for t in range(NT):
                sp.wait_ge(y_stored[t], 16 * GROUPS)

        @block.tensor
        def _(pe):
            def passes(dst, pairs, first=True, last=True):
                n = 0
                for lhs, rhs in pairs:
                    for a, b in ((0, 0), (0, 1), (1, 0)):
                        mm = pe.matmul(dst, lhs[a], rhs[b], start=(n == 0),
                                       stop=(n == 3 * len(pairs) - 1))
                        n += 1
                return mm

            pe.wait_ge(ident_ready, 1)
            pe.wait_ge(setup_v, 6)
            pe.transpose(bank_w[0][:, 0:P], adj_sc[:, :], ident[:, :]).then_inc(adjt_done, 1)
            pe.wait_ge(stage_in[1], 16)
            turned = [bank_p[0], bank_p[1], bank_b[0], bank_b[1]]
            for dc in range(NC):
                for ec in range(NC):
                    mm = pe.transpose(turned[dc][:, ec * P:(ec + 1) * P], x_late[:, ec, dc * P:(dc + 1) * P], ident[:, :])
            mm.then_inc(setup_pe, 1)
            pe.wait_ge(stage_in[2], 16)
            pe.wait_ge(stage_in[0], 32)
            pe.wait_ge(setup_v, 7)
            prod = [bank_w[0], bank_w[1], bank_s[0], bank_s[1]]
            for fc in range(NC):
                for ec in range(NC):
                    mm = pe.matmul(prod[fc][:, :], work[:, ec, fc * P:(fc + 1) * P], x_mid[:, ec, :],
                                   start=(ec == 0), stop=(ec == NC - 1))
            mm.then_inc(setup_pe, 1)

            def b_bank(g, j):
                wait(pe, b_lo, NB * g + j - 1)
                return bank_b[j % 2]

            def adj0(g, t):
                dst = b_bank(g, J_ADJ + t)
                wait(pe, h_ready[0], 4 * g + t + 1)
                for c in range(NC):
                    mm = pe.matmul(dst[:, c * P:(c + 1) * P], h_b[:, t % 2, c * P:(c + 1) * P], adj_norm_t[:, :],
                                   start=(c == 0), stop=(c == NC - 1), skip_group_check=True)
                mm.then_inc(b_done, 1)

            def rows_product(dst, w, ht, t):
                return passes(dst[:, :], [((ht[0][:, c, t * P:(t + 1) * P], ht[1][:, c, t * P:(t + 1) * P]),
                                           (w_hi[w][:, c, :], w_lo[w][:, c, :])) for c in range(NC)])

            def cols_product(dst, w, ht, oc):
                s = slice(oc * P, (oc + 1) * P)
                return passes(dst[:, :], [((w_hi[w][:, c, s], w_lo[w][:, c, s]),
                                           (ht[0][:, c, :], ht[1][:, c, :])) for c in range(NC)])

            HT_B, HT_A = (ht_b_hi, ht_b_lo), (ht_a_hi, ht_a_lo)

            def proj0(g, t):
                dst = b_bank(g, J_PROJ0 + t)
                wait(pe, b_lo, NB * g + J_ADJ + t + 1)
                rows_product(dst, "W0", HT_B, t).then_inc(b_done, 1)

            def turn1(g, t):
                dst = b_bank(g, J_T1 + t)
                wait(pe, h_ready[1], 4 * g + t + 1)
                for c in range(NC):
                    mm = pe.transpose(dst[:, c * P:(c + 1) * P], h_b[:, t % 2, c * P:(c + 1) * P], ident[:, :])
                mm.then_inc(b_done, 1)

            def query1(g, c):
                dst = b_bank(g, J_M1 + c)
                if c == 0:
                    wait(pe, b_lo, NB * g + J_T1 + NT)
                cols_product(dst, "M1", HT_B, c).then_inc(b_done, 1)

            def relation1(g, r):
                dst = b_bank(g, J_REL + r)
                if r == 0:
                    wait(pe, b_lo, NB * g + J_M1 + NC)
                n = 0
                for u in range(2):
                    s = slice((2 * r + u) * P, (2 * r + u + 1) * P)
                    for c in range(NC):
                        for k, q in ((ht_b_hi, qb_hi), (ht_b_hi, qb_lo), (ht_b_lo, qb_hi)):
                            mm = pe.matmul(dst[:, u * P:(u + 1) * P], k[:, c, s], q[:, c, s], start=(n == 0),
                                           stop=(n == 6 * NC - 1), skip_group_check=True)
                            n += 1
                mm.then_inc(b_done, 1)

            def square_sum1(g, r):
                dst = b_bank(g, J_SSQ + r)
                wait(pe, sq_ready, NR * g + r + 1)
                for u in range(2):
                    mm = pe.matmul(dst[:, u:u + 1], rel_sq[:, 2 * r + u, :], ones[:, :], start=(u == 0),
                                   stop=(u == 1), skip_group_check=True)
                mm.then_inc(b_done, 1)

            def value1(g, t):
                rows_product(b_bank(g, J_V1[t]), "V1", HT_B, t).then_inc(b_done, 1)

            def out1(g, t):
                dst = b_bank(g, J_OUT1 + t)
                wait(pe, rello_ready, NR * g + t // 2 + 1)
                wait(pe, b_lo, NB * g + J_V1[t] + 1)
                passes(dst[:, :], [((rel_hi[:, t, :], rel_lo[:, t, :]),
                                    (vb_hi[:, t, :], vb_lo[:, t, :]))]).then_inc(b_done, 1)

            def w_bank(job, t):
                wait(pe, w_lo_s, job - 1)
                return bank_w[t % 2]

            def p_bank(g, j):
                wait(pe, p_lo, NPJ * g + j - 1)
                return bank_p[j % 2]

            def turn(L, g, t):
                dst = w_bank(w_turned(L, g) + t, t)
                wait(pe, h_ready[L], 4 * g + t + 1)
                for c in range(NC):
                    mm = pe.transpose(dst[:, c * P:(c + 1) * P], h_a[:, t % 2, c * P:(c + 1) * P], ident[:, :])
                mm.then_inc(w_done, 1)

            def query(L, g, c):
                dst = p_bank(g, J_Q[L] + c)
                if c == 0:
                    wait(pe, w_lo_s, w_turned(L, g) + NT)
                cols_product(dst, f"Q{L}", HT_A, c).then_inc(p_done, 1)

            def key(L, g, c):
                cols_product(p_bank(g, J_K[L] + c), f"K{L}", HT_A, c).then_inc(p_done, 1)

            def value(L, g, t):
                rows_product(p_bank(g, J_V[L] + t), f"V{L}", HT_A, t).then_inc(p_done, 1)

            def scores(L, g, t):
                wait(pe, s_read, NS * g + J_S[L] + t)
                if t == 0:
                    wait(pe, p_lo, NPJ * g + J_K[L] + NC)
                s = slice(t * P, (t + 1) * P)
                for j in range(NJ):
                    for r in range(2):
                        f = slice(r * HD, (r + 1) * HD)
                        dst = bank_s[r][:, j * P:(j + 1) * P]
                        for n, (a, b) in enumerate(((q_hi, k_hi), (q_hi, k_lo), (q_lo, k_hi))):
                            mm = pe.matmul(dst, a[f, j, s], b[f, j, s], start=(j == 0 and n == 0),
                                           stop=(n == 2), skip_group_check=True)
                mm.then_inc(s_done, 1)

            def turn_weights(L, g, t):
                dst = w_bank(w_attended(L, g) + J_PT[t], J_PT[t])
                if L == 2:
                    wait(pe, prob_ready, 4 * g + t + 1)
                else:
                    wait(pe, exp_ready[3], 4 * g + t + 1)
                for j in range(NJ):
                    mm = pe.transpose(dst[:, j * P:(j + 1) * P], work[:, t, j * P:(j + 1) * P], ident[:, :])
                mm.then_inc(w_done, 1)

            def attend(L, g, t):
                dst = w_bank(w_attended(L, g) + J_PV[t], J_PV[t])
                wait(pe, w_lo_s, w_attended(L, g) + J_PT[t] + 1)
                for placed in (vbd_ready, vbd_act_ready):
                    wait(pe, placed, 8 * g + (4 if L == 3 else 0) + t + 1)
                for j in range(NJ):
                    for b in range(B2):
                        q = slice(b * N, (b + 1) * N)
                        v = [v_bd[:, t, s, b, j, :] for s in range(2)]
                        p = [pt[:, t % 2, j, q] for pt in (pt_hi, pt_lo)]
                        for n, (sv, sp_) in enumerate(((0, 0), (0, 1), (1, 0))):
                            if L == 2:
                                mm = pe.matmul(dst[:, j * P + b * N:j * P + (b + 1) * N], v[sv], p[sp_],
                                               start=(j == 0 and b == 0 and n == 0), stop=(n == 2),
                                               skip_group_check=True)
                            else:
                                mm = pe.matmul(dst[q, j * P:(j + 1) * P], p[sp_], v[sv],
                                               start=(j == 0 and n == 0), stop=(n == 2),
                                               skip_group_check=True)
                mm.then_inc(w_done, 1)

            def project2(g, t):
                dst = p_bank(g, J_PR2 + t)
                wait(pe, w_lo_s, w_attended(2, g) + J_PV[t] + 1)
                rows_product(dst, "P2", HT_A, t).then_inc(p_done, 1)

            def body(gb, ga, gp):
                a, b, p = ga is not None, gb is not None, gp is not None
                if p:
                    turn_weights(3, gp, 0)
                    turn_weights(3, gp, 1)
                for t in range(NT):
                    if a:
                        query(2, ga, t)
                    if p:
                        attend(3, gp, t)
                        if t < 2:
                            turn_weights(3, gp, t + 2)
                for t in range(NT):
                    if a:
                        key(2, ga, t)
                    if b:
                        adj0(gb, t)
                if b:
                    proj0(gb, 0)
                for t in range(NT):
                    if a:
                        scores(2, ga, t)
                        value(2, ga, t)
                    if b and t % 2:
                        proj0(gb, 1 + t // 2)
                if a:
                    turn_weights(2, ga, 0)
                    turn_weights(2, ga, 1)
                if b:
                    proj0(gb, 3)
                for t in range(NT):
                    if a:
                        attend(2, ga, t)
                        if t < 2:
                            turn_weights(2, ga, t + 2)
                    if b and t < 3:
                        turn1(gb, t)
                for t in range(NT):
                    if a:
                        project2(ga, t)
                    if b:
                        turn1(gb, 3) if t == 0 else query1(gb, t - 1)
                if b:
                    query1(gb, 3)
                if a:
                    turn(3, ga, 0)
                    turn(3, ga, 1)
                if b:
                    relation1(gb, 0)
                    relation1(gb, 1)
                    value1(gb, 0)
                if a:
                    turn(3, ga, 2)
                if b:
                    square_sum1(gb, 0)
                    square_sum1(gb, 1)
                if a:
                    turn(3, ga, 3)
                if b:
                    for t in range(1, NT):
                        value1(gb, t)
                if a:
                    query(3, ga, 0)
                    query(3, ga, 1)
                if b:
                    out1(gb, 0)
                    out1(gb, 1)
                if a:
                    query(3, ga, 2)
                    query(3, ga, 3)
                    for c in range(NC):
                        key(3, ga, c)
                if b:
                    out1(gb, 2)
                    out1(gb, 3)
                for t in range(NT):
                    if a:
                        scores(3, ga, t)
                        value(3, ga, t)
                    if b:
                        turn(2, gb, t)

            pe.wait_ge(conv_lo, len(converted) + 2 * NC)
            body(0, None, None)
            body(1, 0, None)
            with pe.Fori(2, GROUPS) as i:
                body(i, i - 1, i - 2)
            body(None, GROUPS - 1, GROUPS - 2)
            body(None, None, GROUPS - 1)

        @block.scalar
        def _(act):
            def hi_weights(name):
                slot = {n: s for n, _, s in loads}[name]
                wait(act, stage_in[slot], 16 * slot_turn[name])
                act.activation(w_hi[name][:, :, :], stage[slot][:, :, :], ACT.Copy, scale=WS).then_inc(conv_hi, 1)

            hi_weights("W0")
            turned = [bank_p[0], bank_p[1], bank_b[0], bank_b[1]]
            act.wait_ge(setup_pe, 1)
            for c in range(NC):
                act.activation(w_hi["V1"][:, c, :], turned[c][:, :], ACT.Copy, scale=WS).then_inc(conv_hi, 1)
            prod = [bank_w[0], bank_w[1], bank_s[0], bank_s[1]]
            act.wait_ge(setup_pe, 2)
            for c in range(NC):
                act.activation(w_hi["M1"][:, c, :], prod[c][:, :], ACT.Copy, scale=WS).then_inc(conv_hi, 1)
            for name in converted[1:]:
                hi_weights(name)
            act.wait_ge(setup_v, 11)

            def relu(L, src, h, t, g, free_sem, free_at):
                wait(act, nbias_ready[L], 4 * g + t + 1)
                wait(act, free_sem, free_at)
                act.activation(h[:, t % 2, :], src[:, t, :], ACT.Relu, bias=nbias[:, L, t:t + 1],
                               scale=rstd[:, L, t:t + 1]).then_inc(h_ready[L], 1)

            def relu0(g, t):
                relu(0, x_in, h_b, t, g, b_done, NB * g + (J_T1 + t + 3 - NB if t < 2 else J_ADJ + t - 1))

            def relu1(g, t):
                relu(1, x_in, h_b, t, g, b_done, NB * g + (J_ADJ + t + 3 if t < 2 else J_T1 + t - 1))

            def relu2(g, t):
                relu(2, x_mid, h_a, t, g, w_done, w_turned(3, g - 1) + t + 3 if t < 2 else w_turned(2, g) + t - 1)

            def relu3(g, t):
                relu(3, x_late, h_a, t, g, w_done, w_turned(2, g) + t + 3 if t < 2 else w_turned(3, g) + t - 1)

            def tile_cols(buf, t):
                return buf[:, :, t * P:(t + 1) * P]

            def chunks(bank):
                return bank[:, :].rearrange("p (c r) -> p c r", c=NC)

            def b_read(g, j, dst, shaped=False, **kw):
                wait(act, b_done, NB * g + j + 1)
                src = bank_b[j % 2]
                act.activation(dst, chunks(src) if shaped else src[:, :], ACT.Copy, **kw).then_inc(b_hi, 1)

            def adj0_hi(g, t):
                b_read(g, J_ADJ + t, tile_cols(ht_b_hi, t), True)

            def turn1_hi(g, t):
                b_read(g, J_T1 + t, tile_cols(ht_b_hi, t), True)

            def query1_hi(g, c):
                b_read(g, J_M1 + c, qb_hi[:, c, :])

            def value1_hi(g, t):
                b_read(g, J_V1[t], vb_hi[:, t, :])

            def relation1_hi(g, r):
                wait(act, b_lo, NB * g + J_REL + r + 1)
                s = slice(2 * r, 2 * r + 2)
                act.activation(rel_hi[:, s, :], rel[:, s, :], ACT.Copy).then_inc(relhi_ready, 1)
                act.activation(rel_sq[:, s, :], rel[:, s, :], ACT.Square).then_inc(sq_ready, 1)

            def turn_hi(L, g, t):
                wait(act, w_done, w_turned(L, g) + t + 1)
                act.activation(tile_cols(ht_a_hi, t), chunks(bank_w[t % 2]), ACT.Copy).then_inc(w_hi_s, 1)

            def query_key_hi(L, g, c, key):
                j = (J_K if key else J_Q)[L] + c
                wait(act, p_done, NPJ * g + j + 1)
                dst = (k_hi if key else q_hi)[:, c, :]
                if L == 3:
                    act.activation(dst, bank_p[j % 2][:, :], ACT.Identity,
                                   bias=(bias_k if key else bias_q)[:, c:c + 1]).then_inc(p_hi, 1)
                else:
                    act.activation(dst, bank_p[j % 2][:, :], ACT.Copy).then_inc(p_hi, 1)

            def value_hi(L, g, t):
                j = J_V[L] + t
                wait(act, p_done, NPJ * g + j + 1)
                wait(act, vbd_ready, 8 * g + (4 if L == 3 else 0) + t - 1)
                act.activation(v_nat[:, t % 2, 0, :], bank_p[j % 2][:, :], ACT.Copy).then_inc(p_hi, 1)

            def value_place(L, g, t):
                wait(act, p_lo, NPJ * g + J_V[L] + t + 1)
                for r in range(2):
                    src = v_nat[N:P, t % 2, :, :].rearrange("p s (j r d) -> p s j r d", j=NJ, r=2)
                    cp = act.activation(v_bd[r * N:(r + 1) * N, t, :, 1, :, r * HD:(r + 1) * HD], src[:, :, :, r, :],
                                        ACT.Copy)
                cp.then_inc(vbd_act_ready, 1)

            def exp(L, g, t):
                wait(act, sub_ready[L], 4 * g + t + 1)
                act.activation(work[:, t, :], work[:, t, :], ACT.Exp, scale=SCALE / (WS * WS)).then_inc(exp_ready[L], 1)

            def weights_hi(L, g, t):
                wait(act, w_done, w_attended(L, g) + J_PT[t] + 1)
                act.activation(pt_hi[:, t % 2, :, :], chunks(bank_w[J_PT[t] % 2]), ACT.Copy, scale=PS).then_inc(w_hi_s, 1)

            def attn2_hi(g, t):
                wait(act, w_done, w_attended(2, g) + J_PV[t] + 1)
                act.activation(tile_cols(ht_a_hi, t), chunks(bank_w[J_PV[t] % 2]), ACT.Copy, scale=1.0 / PS).then_inc(w_hi_s, 1)

            def body(gb, ga, gp):
                a, b, p = ga is not None, gb is not None, gp is not None
                if p:
                    weights_hi(3, gp, 0)
                    weights_hi(3, gp, 1)
                for t in range(NT):
                    if a:
                        query_key_hi(2, ga, t, False)
                    if p and t < 2:
                        weights_hi(3, gp, t + 2)
                    if b and t >= 2:
                        relu0(gb, t - 2)
                for t in range(NT):
                    if a:
                        query_key_hi(2, ga, t, True)
                    if b:
                        adj0_hi(gb, t)
                        if t < 2:
                            relu0(gb, t + 2)
                for t in range(NT):
                    if a:
                        value_hi(2, ga, t)
                        value_place(2, ga, t)
                        exp(2, ga, t)
                    if b and t % 2:
                        relu1(gb, t // 2)
                if a:
                    weights_hi(2, ga, 0)
                    weights_hi(2, ga, 1)
                for t in range(NT):
                    if a:
                        attn2_hi(ga, t)
                        if t < 2:
                            weights_hi(2, ga, t + 2)
                    if b and t < 3:
                        turn1_hi(gb, t)
                        if t < 2:
                            relu1(gb, t + 2)
                if b:
                    turn1_hi(gb, 3)
                for t in range(NT):
                    if b:
                        query1_hi(gb, t)
                    if a and t in (1, 2):
                        relu3(ga, t - 1)
                if a:
                    turn_hi(3, ga, 0)
                    relu3(ga, 2)
                    turn_hi(3, ga, 1)
                if b:
                    relation1_hi(gb, 0)
                    relation1_hi(gb, 1)
                if a:
                    relu3(ga, 3)
                if b:
                    value1_hi(gb, 0)
                if a:
                    turn_hi(3, ga, 2)
                    turn_hi(3, ga, 3)
                if b:
                    for t in range(1, NT):
                        value1_hi(gb, t)
                if a:
                    for c in range(NC):
                        query_key_hi(3, ga, c, False)
                for c in range(NC):
                    if a:
                        query_key_hi(3, ga, c, True)
                    if b and c < 2:
                        relu2(gb, c)
                for t in range(NT):
                    if a:
                        value_hi(3, ga, t)
                    if b:
                        turn_hi(2, gb, t)
                        if t < 2:
                            relu2(gb, t + 2)
                    if a:
                        value_place(3, ga, t)
                        exp(3, ga, t)

            body(0, None, None)
            body(1, 0, None)
            with act.Fori(2, GROUPS) as i:
                body(i, i - 1, i - 2)
            body(None, GROUPS - 1, GROUPS - 2)
            body(None, None, GROUPS - 1)

        @block.vector
        def _(dve):
            dve.wait_ge(adj_in, 16 * B2)
            dve.tensor_reduce(deg[:, 0:1], adj_row[:, :], AX.X, ALU.add).then_inc(setup_v, 1)
            dve.wait_ge(const_ready, 1)
            for b in range(B2):
                dve.tensor_copy(adj_bd[b * N:(b + 1) * N, b * N:(b + 1) * N], adj_row[b * N:(b + 1) * N, :])\
                   .then_inc(setup_v, 1)
            dve.wait_ge(setup_v, 3)
            dve.tensor_scalar(deg[:, 1:2], deg[:, 0:1], TINY, None, ALU.max).then_inc(setup_v, 1)
            dve.tensor_scalar(deg[:, 2:3], deg[:, 0:1], 0.0, None, ALU.is_gt).then_inc(setup_v, 1)
            dve.wait_ge(setup_v, 5)
            dve.wait_ge(setup_p, 1)
            dve.tensor_scalar(adj_sc[:, :], adj_bd[:, :], deg[:, 3:4], deg[:, 2:3], ALU.mult, ALU.mult)\
               .then_inc(setup_v, 1)
            dve.wait_ge(adjt_done, 1)
            dve.tensor_scalar(adj_norm_t[:, :], bank_w[0][:, 0:P], deg[:, 3:4], deg[:, 2:3], ALU.mult, ALU.mult)\
               .then_inc(setup_v, 1)
            dve.tensor_scalar(mask2[:, :], adj_row[:, :], 0.0, -3e38, ALU.is_equal, ALU.mult).then_inc(setup_v, 1)
            dve.tensor_scalar(mask3[:, :], adj_row[:, :], 0.0, -1e9 / SCALE * WS * WS, ALU.is_equal, ALU.mult)\
               .then_inc(setup_v, 1)
            dve.wait_ge(col_in, 32)
            dve.tensor_scalar(bias_q[:, :], bias_q[:, :], WS, None, ALU.mult).then_inc(setup_v, 1)
            dve.tensor_scalar(bias_k[:, :], bias_k[:, :], WS, None, ALU.mult).then_inc(setup_v, 1)

            slots = {n: s for n, _, s in loads}
            turned = [bank_p[0], bank_p[1], bank_b[0], bank_b[1]]
            prod = [bank_w[0], bank_w[1], bank_s[0], bank_s[1]]

            def lo_weights(n, dst, src, hi):
                dve.wait_ge(conv_hi, n)
                dve.scalar_tensor_tensor(out=dst, in0=src, scalar=WS, in1=hi, op0=ALU.mult, op1=ALU.subtract)\
                   .then_inc(conv_lo, 1)

            def lo_flat(name):
                lo_weights(conv_count[name], w_lo[name][:, :, :], stage[slots[name]][:, :, :], w_hi[name][:, :, :])

            lo_flat("W0")
            for c in range(NC):
                lo_weights(2 + c, w_lo["V1"][:, c, :], turned[c][:, :], w_hi["V1"][:, c, :])
            for c in range(NC):
                lo_weights(2 + NC + c, w_lo["M1"][:, c, :], prod[c][:, :], w_hi["M1"][:, c, :])
            for name in converted[1:]:
                lo_flat(name)
            dve.wait_ge(setup_v, 11)
            dve.wait_ge(small_in, 16 * 5)

            def stats(L, src, g, t):
                dve.bn_stats(bn6[:, L, t, :], src[:, t, :]).then_inc(stats_done[L], 1)
                wait_apart(dve, stats_done[L], 4 * g + t + 1, passed_v)
                dve.bn_aggr(mean_var[:, L, t, :], bn6[:, L, t, :]).then_inc(mv_ready[L], 1)

            def tile_cols(buf, t):
                return buf[:, :, t * P:(t + 1) * P]

            def chunks(bank):
                return bank[:, :].rearrange("p (c r) -> p c r", c=NC)

            def lo(dst, src, hi, sem_, scale=None):
                if scale is None:
                    dve.tensor_tensor(dst, src, hi, ALU.subtract).then_inc(sem_, 1)
                else:
                    dve.scalar_tensor_tensor(out=dst, in0=src, scalar=scale, in1=hi, op0=ALU.mult,
                                             op1=ALU.subtract).then_inc(sem_, 1)

            def norm0(g, t):
                wait(dve, x_loaded[t], 16 * g + 16)
                stats(0, x_in, g, t)

            def adj0_lo(g, t):
                wait(dve, b_hi, NB_HI * g + t + 1)
                lo(tile_cols(ht_b_lo, t), chunks(bank_b[(J_ADJ + t) % 2]), tile_cols(ht_b_hi, t), b_lo)

            def residual0(g, t):
                wait(dve, b_done, NB * g + J_PROJ0 + t + 1)
                wait(dve, xb0_ready, 4 * g + t + 1)
                dve.scalar_tensor_tensor(out=x_in[:, t, :], in0=bank_b[(J_PROJ0 + t) % 2][:, :], scalar=1.0 / WS,
                                         in1=x_in[:, t, :], op0=ALU.mult, op1=ALU.add).then_inc(b_lo, 1)
                wait(dve, b_lo, NB * g + J_PROJ0 + t + 1)
                stats(1, x_in, g, t)

            def turn1_lo(g, t):
                wait(dve, b_hi, NB_HI * g + 4 + t + 1)
                lo(tile_cols(ht_b_lo, t), chunks(bank_b[(J_T1 + t) % 2]), tile_cols(ht_b_hi, t), b_lo)

            def query1_lo(g, c):
                wait(dve, b_hi, NB_HI * g + 8 + c + 1)
                lo(qb_lo[:, c, :], bank_b[(J_M1 + c) % 2][:, :], qb_hi[:, c, :], b_lo)

            def value1_lo(g, t):
                wait(dve, b_hi, NB_HI * g + 12 + t + 1)
                lo(vb_lo[:, t, :], bank_b[J_V1[t] % 2][:, :], vb_hi[:, t, :], b_lo)

            def relation1(g, r):
                wait(dve, b_done, NB * g + J_REL + r + 1)
                dve.scalar_tensor_tensor(out=rel[:, 2 * r:2 * r + 2, :],
                                         in0=bank_b[(J_REL + r) % 2][:, 0:2 * P].rearrange("p (u k) -> p u k", u=2),
                                         scalar=1.0 / (WS * WS), in1=adj_bd[:, :].unsqueeze(1).broadcast_to((P, 2, P)),
                                         op0=ALU.mult, op1=ALU.mult).then_inc(b_lo, 1)

            def relation1_lo(g, r):
                wait(dve, relhi_ready, NR * g + r + 1)
                s = slice(2 * r, 2 * r + 2)
                dve.tensor_tensor(rel_lo[:, s, :], rel[:, s, :], rel_hi[:, s, :], ALU.subtract)\
                   .then_inc(rello_ready, 1)

            def ssq1(g, r):
                wait(dve, b_done, NB * g + J_SSQ + r + 1)
                dve.tensor_scalar(rel_ssq[:, 2 * r:2 * r + 2], bank_b[(J_SSQ + r) % 2][:, 0:2], WS * WS, None,
                                  ALU.mult).then_inc(b_lo, 1)

            def residual1(g, t):
                wait(dve, b_done, NB * g + J_OUT1 + t + 1)
                wait(dve, rn_ready, NR * g + t // 2 + 1)
                wait(dve, xo_ready, 4 * g - 3 + t)
                dve.scalar_tensor_tensor(out=x_mid[:, t, :], in0=bank_b[(J_OUT1 + t) % 2][:, :],
                                         scalar=rel_rn[:, t:t + 1], in1=x_in[:, t, :], op0=ALU.mult, op1=ALU.add)\
                   .then_inc(b_lo, 1)
                wait(dve, b_lo, NB * g + J_OUT1 + t + 1)
                stats(2, x_mid, g, t)

            def turn_lo(L, g, t):
                wait(dve, w_hi_s, w_turned_hi(L, g) + t + 1)
                lo(tile_cols(ht_a_lo, t), chunks(bank_w[t % 2]), tile_cols(ht_a_hi, t), w_lo_s)

            def query_key_lo(L, g, c, key):
                j = (J_K if key else J_Q)[L] + c
                wait(dve, p_hi, NP_HI * g + (HI_K if key else HI_Q)[L] + c + 1)
                dst, hi = ((k_lo, k_hi) if key else (q_lo, q_hi))
                if L == 3:
                    dve.scalar_tensor_tensor(out=dst[:, c, :], in0=bank_p[j % 2][:, :],
                                             scalar=(bias_k if key else bias_q)[:, c:c + 1], in1=hi[:, c, :],
                                             op0=ALU.add, op1=ALU.subtract).then_inc(p_lo, 1)
                else:
                    lo(dst[:, c, :], bank_p[j % 2][:, :], hi[:, c, :], p_lo)

            def value_lo(L, g, t):
                j = J_V[L] + t
                wait(dve, p_hi, NP_HI * g + HI_V[L] + t + 1)
                lo(v_nat[:, t % 2, 1, :], bank_p[j % 2][:, :], v_nat[:, t % 2, 0, :], p_lo)
                wait(dve, p_lo, NPJ * g + j + 1)
                for r in range(2):
                    src = v_nat[0:N, t % 2, :, :].rearrange("p s (j r d) -> p s j r d", j=NJ, r=2)
                    cp = dve.tensor_copy(v_bd[r * N:(r + 1) * N, t, :, 0, :, r * HD:(r + 1) * HD], src[:, :, :, r, :])
                cp.then_inc(vbd_ready, 1)

            def per_head(buf, t):
                return buf[:, t, :].rearrange("p (h k) -> p h k", h=H)

            def scores(L, g, t):
                mask = mask2 if L == 2 else mask3
                wait(dve, s_done, NS * g + J_S[L] + t + 1)
                for r in range(2):
                    for b in range(B2):
                        q = slice(b * N, (b + 1) * N)
                        dst = work[q, t, :].rearrange("p (j r k) -> p j r k", j=NJ, r=2)[:, :, r, :]
                        src = bank_s[r][q, :].rearrange("p (j k) -> p j k", j=NJ)[:, :, q]
                        tt = dve.tensor_tensor(dst, src, mask[q, :].unsqueeze(1).broadcast_to((N, NJ, N)), ALU.add)
                tt.then_inc(s_read, 1)

            def softmax_shift(L, g, t):
                wait(dve, s_read, NS * g + J_S[L] + t + 1)
                dve.tensor_reduce(row_max[:, t, :], per_head(work, t), AX.X, ALU.max).then_inc(max_ready[L], 1)
                wait(dve, max_ready[L], 4 * g + t + 1)
                dve.tensor_tensor(per_head(work, t), per_head(work, t),
                                  row_max[:, t, :].unsqueeze(2).broadcast_to((P, H, N)), ALU.subtract)\
                   .then_inc(sub_ready[L], 1)

            def softmax_sum(L, g, t):
                wait(dve, exp_ready[L], 4 * g + t + 1)
                dve.tensor_reduce(row_sum[:, t, :], per_head(work, t), AX.X, ALU.add).then_inc(sum_ready[L], 1)
                wait(dve, sum_ready[L], 4 * g + t + 1)
                dve.reciprocal(row_inv[:, t, :], row_sum[:, t, :]).then_inc(inv_ready[L], 1)

            def weights_lo(L, g, t):
                wait(dve, w_hi_s, w_attended_hi(L, g) + (J_PT[t] if L == 2 else t) + 1)
                lo(pt_lo[:, t % 2, :, :], chunks(bank_w[J_PT[t] % 2]), pt_hi[:, t % 2, :, :], w_lo_s, PS)

            def attn2_lo(g, t):
                wait(dve, w_hi_s, w_attended_hi(2, g) + J_PV[t] + 1)
                lo(tile_cols(ht_a_lo, t), chunks(bank_w[J_PV[t] % 2]), tile_cols(ht_a_hi, t), w_lo_s, 1.0 / PS)

            def project2(g, t):
                j = J_PR2 + t
                wait(dve, p_done, NPJ * g + j + 1)
                dve.scalar_tensor_tensor(out=work[:, t, :], in0=bank_p[j % 2][:, :], scalar=1.0 / (WS * WS),
                                         in1=biasp[:, :], op0=ALU.mult, op1=ALU.add).then_inc(p_lo, 1)
                wait(dve, p_lo, NPJ * g + j + 1)
                stats(4, work, g, t)

            def residual2(g, t):
                wait(dve, xo_ready, 4 * g + t + 1)
                wait(dve, mv_ready[4], 4 * g + t + 1)
                dve.scalar_tensor_tensor(out=work[:, t, :], in0=work[:, t, :], scalar=mean_var[:, 4, t, 0:1],
                                         in1=gamma[:, :], op0=ALU.subtract, op1=ALU.mult).then_inc(og_ready, 1)
                wait(dve, og_ready, 4 * g + t + 1)
                wait(dve, rstd_ready[4], 4 * g + t + 1)
                dve.scalar_tensor_tensor(out=x_late[:, t, :], in0=work[:, t, :], scalar=rstd[:, 4, t:t + 1],
                                         in1=x_late[:, t, :], op0=ALU.mult, op1=ALU.add).then_inc(x3_ready, 1)
                wait(dve, x3_ready, 4 * g + t + 1)
                stats(3, x_late, g, t)

            def result(g, t):
                job = w_attended(3, g) + J_PV[t] + 1
                wait(dve, w_done, job)
                wait(dve, inv_ready[3], 4 * g + t + 1)
                dve.tensor_tensor(per_head(work, t), bank_w[J_PV[t] % 2][:, :].rearrange("p (h k) -> p h k", h=H),
                                  row_inv[:, t, :].unsqueeze(2).broadcast_to((P, H, HD)), ALU.mult).then_inc(w_lo_s, 1)
                wait(dve, w_lo_s, job)
                wait(dve, xb3_ready, 4 * g + t + 1)
                dve.scalar_tensor_tensor(out=x_late[:, t, :], in0=work[:, t, :], scalar=1.0 / (WS * PS),
                                         in1=x_late[:, t, :], op0=ALU.mult, op1=ALU.add).then_inc(y_ready, 1)

            def body(gb, ga, gp):
                a, b, p = ga is not None, gb is not None, gp is not None
                if p:
                    weights_lo(3, gp, 0)
                    weights_lo(3, gp, 1)
                for t in range(NT):
                    if a:
                        query_key_lo(2, ga, t, False)
                    if p:
                        result(gp, t)
                        if t < 2:
                            weights_lo(3, gp, t + 2)
                    if b:
                        norm0(gb, t)
                for t in range(NT):
                    if a:
                        query_key_lo(2, ga, t, True)
                    if b:
                        adj0_lo(gb, t)
                if b:
                    residual0(gb, 0)
                for t in range(NT):
                    if a:
                        scores(2, ga, t)
                        softmax_shift(2, ga, t)
                        value_lo(2, ga, t)
                        if t:
                            softmax_sum(2, ga, t - 1)
                    if b and t % 2:
                        residual0(gb, 1 + t // 2)
                if a:
                    softmax_sum(2, ga, NT - 1)
                    weights_lo(2, ga, 0)
                    weights_lo(2, ga, 1)
                if b:
                    residual0(gb, 3)
                for t in range(NT):
                    if a:
                        attn2_lo(ga, t)
                        if t < 2:
                            weights_lo(2, ga, t + 2)
                    if b and t < 3:
                        turn1_lo(gb, t)
                for t in range(NT):
                    if a:
                        project2(ga, t)
                    if b:
                        turn1_lo(gb, 3) if t == 0 else query1_lo(gb, t - 1)
                    if a and t:
                        residual2(ga, t - 1)
                if b:
                    query1_lo(gb, 3)
                if a:
                    turn_lo(3, ga, 0)
                    residual2(ga, 3)
                    turn_lo(3, ga, 1)
                if b:
                    relation1(gb, 0)
                    relation1(gb, 1)
                    relation1_lo(gb, 0)
                    relation1_lo(gb, 1)
                    value1_lo(gb, 0)
                if a:
                    turn_lo(3, ga, 2)
                if b:
                    ssq1(gb, 0)
                    ssq1(gb, 1)
                if a:
                    turn_lo(3, ga, 3)
                if b:
                    for t in range(1, NT):
                        value1_lo(gb, t)
                if a:
                    query_key_lo(3, ga, 0, False)
                    query_key_lo(3, ga, 1, False)
                if b:
                    residual1(gb, 0)
                    residual1(gb, 1)
                if a:
                    query_key_lo(3, ga, 2, False)
                    query_key_lo(3, ga, 3, False)
                    for c in range(NC):
                        query_key_lo(3, ga, c, True)
                if b:
                    residual1(gb, 2)
                    residual1(gb, 3)
                for t in range(NT):
                    if a:
                        scores(3, ga, t)
                        softmax_shift(3, ga, t)
                        value_lo(3, ga, t)
                    if b:
                        turn_lo(2, gb, t)
                    if a and t:
                        softmax_sum(3, ga, t - 1)
                if a:
                    softmax_sum(3, ga, NT - 1)

            body(0, None, None)
            body(1, 0, None)
            with dve.Fori(2, GROUPS) as i:
                body(i, i - 1, i - 2)
            body(None, GROUPS - 1, GROUPS - 2)
            body(None, None, GROUPS - 1)

        @block.gpsimd
        def _(pool):
            pool.memset(ident[:, :], 0.0).then_inc(zero_ready, 1)
            pool.memset(adj_bd[:, :], 0.0).then_inc(const_ready, 1)
            pool.memset(neg_half[:, :], -0.5).then_inc(zero_ready, 1)
            pool.memset(ones[:, :], 1.0).then_inc(zero_ready, 1)
            pool.memset(v_bd[:, :, :, :, :, :], 0.0).then_inc(zero_ready, 1)
            pool.wait_ge(zero_ready, 4)
            pool.affine_select(out=ident[:, :], in_=ident[:, :], compare_op=ALU.not_equal, fill=1.0, base=0,
                               pattern=[[-1, P]], channel_multiplier=1).then_inc(ident_ready, 1)
            pool.wait_ge(setup_v, 4)
            pool.tensor_tensor(deg[:, 3:4], deg[:, 1:2], neg_half[:, :], ALU.pow).then_inc(setup_p, 1)
            pool.wait_ge(small_in, 16 * 5)

            def root(L, g, t, bias=True):
                wait_apart(pool, mv_ready[L], 4 * g + t + 1, passed_p)
                pool.tensor_scalar(var_eps[:, L, t:t + 1], mean_var[:, L, t, 1:2], LN_EPS, None, ALU.add)\
                    .then_inc(ve_ready[L], 1)
                wait(pool, ve_ready[L], 4 * g + t + 1)
                pool.tensor_tensor(rstd[:, L, t:t + 1], var_eps[:, L, t:t + 1], neg_half[:, :], ALU.pow)\
                    .then_inc(rstd_ready[L], 1)
                if bias:
                    wait_apart(pool, rstd_ready[L], 4 * g + t + 1, passed_p)
                    pool.tensor_scalar(nbias[:, L, t:t + 1], rstd[:, L, t:t + 1], mean_var[:, L, t, 0:1], -1.0,
                                       ALU.mult, ALU.mult).then_inc(nbias_ready[L], 1)

            def add_rows(dst, a, b, sem_):
                pool.tensor_tensor(dst, a, b, ALU.add).then_inc(sem_, 1)

            def normalise2(g, t):
                wait(pool, inv_ready[2], 4 * g + t + 1)
                heads = work[:, t, :].rearrange("p (h k) -> p h k", h=H)
                pool.tensor_tensor(heads, heads, row_inv[:, t, :].unsqueeze(2).broadcast_to((P, H, N)),
                                   ALU.mult).then_inc(prob_ready, 1)

            def body(gb, ga, gp):
                a, b, p = ga is not None, gb is not None, gp is not None
                if b:
                    for t in range(NT):
                        root(0, gb, t)
                    for t in range(NT):
                        wait(pool, h_ready[0], 4 * gb + t + 1)
                        add_rows(x_in[:, t, :], x_in[:, t, :], bias0[:, :], xb0_ready)
                    root(1, gb, 0)
                for t in range(NT):
                    if a:
                        normalise2(ga, t)
                    if b and t and t < 3:
                        root(1, gb, t)
                if b:
                    root(1, gb, 3)
                if a:
                    for t in range(NT):
                        wait(pool, b_lo, NB * ga + J_OUT1 + t + 1)
                        wait(pool, y_stored[t], 16 * ga)
                        add_rows(x_late[:, t, :], x_mid[:, t, :], beta[:, :], xbeta_ready)
                    for t in range(NT):
                        wait(pool, p_lo, NPJ * ga + J_PR2 + t + 1)
                        wait(pool, xbeta_ready, 4 * ga + t + 1)
                        add_rows(x_late[:, t, :], x_late[:, t, :], work[:, t, :], xo_ready)
                        root(4, ga, t, bias=False)
                        if t:
                            root(3, ga, t - 1)
                    root(3, ga, NT - 1)
                if b:
                    for r in range(NR):
                        wait(pool, b_lo, NB * gb + J_SSQ + r + 1)
                        pool.tensor_tensor(rel_rn[:, 2 * r:2 * r + 2], rel_ssq[:, 2 * r:2 * r + 2],
                                           neg_half[:, :].broadcast_to((P, 2)), ALU.pow).then_inc(rn_ready, 1)
                if a:
                    for t in range(NT):
                        wait(pool, h_ready[3], 4 * ga + t + 1)
                        add_rows(x_late[:, t, :], x_late[:, t, :], biasv[:, :], xb3_ready)
                if b:
                    for t in range(NT):
                        root(2, gb, t)

            body(0, None, None)
            body(1, 0, None)
            with pool.Fori(2, GROUPS) as i:
                body(i, i - 1, i - 2)
            body(None, GROUPS - 1, GROUPS - 2)


_INS = ['x', 'adj', 'L0_gnn_weight', 'L0_gnn_bias', 'L1_gnn_Wq', 'L1_gnn_Wk', 'L1_gnn_Wv', 'L2_gnn_w_qkv',
        'L2_gnn_w_proj', 'L2_gnn_b_proj', 'L2_gnn_ln_gamma', 'L2_gnn_ln_beta', 'L3_gnn_Wq', 'L3_gnn_bq',
        'L3_gnn_Wk', 'L3_gnn_bk', 'L3_gnn_Wv', 'L3_gnn_bv']
_OUTS = [((128, 64, 512), 'float32')]


def kernel(**inputs):
    import numpy as _np
    import concourse.bacc as _bacc
    from concourse import mybir as _mybir
    from concourse.bass_utils import run_bass_kernel_spmd as _run

    nc = _bacc.Bacc("TRN2", target_bir_lowering=False, num_devices=1)
    arrays, args = {}, []
    for name in _INS:
        a = _np.ascontiguousarray(inputs[name])
        arrays[f"in_{name}_dram"] = a
        args.append(nc.dram_tensor(f"in_{name}_dram", a.shape, _mybir.dt.from_np(a.dtype), kind="ExternalInput").ap())
    for i, (shape, dtype) in enumerate(_OUTS):
        dt = _mybir.dt.from_np(_np.dtype(dtype))
        args.append(nc.dram_tensor(f"out_{i}_dram", shape, dt, kind="ExternalOutput").ap())
    gnn_kernel(nc, *args)
    r = _run(nc, [arrays], core_ids=[0])
    got = tuple(r.results[0][f"out_{i}_dram"] for i in range(len(_OUTS)))
    return got[0]
```

```python
from contextlib import ExitStack

import concourse.bass as bass
from concourse import mybir

F32, F16 = mybir.dt.float32, mybir.dt.float16
ALU = mybir.AluOpType
ACT = mybir.ActivationFunctionType
AX = mybir.AxisListType

P = 128
LN_EPS = 1e-5
WS = 16.0
PS = 64.0
TINY = 1e-30


def counts(value):
    return not isinstance(value, int) or value > 0


def gnn_kernel(nc, x, adj, w0, b0, wq1, wk1, wv1, wqkv2, wp2, bp2, gam2, bet2,
               wq3, bq3, wk3, bk3, wv3, bv3, out):
    G, N, D = x.shape
    H = 8
    HD = D // H
    NT = 4
    NC = D // P
    ROWS = NT * P
    GROUPS = G * N // ROWS
    B2 = P // N
    NJ = H // 2
    assert N == HD == 64 and D == 512 and B2 == 2 and NC == NT == 4
    SCALE = HD ** -0.5
    x_rows = x.rearrange("g n d -> (g n) d")
    y_rows = out.rearrange("g n d -> (g n) d")

    with ExitStack() as ctx:
        def sb(name, shape, dt):
            return ctx.enter_context(nc.sbuf_tensor(name, shape, dt))

        def bank(name):
            return ctx.enter_context(nc.psum_tensor(name, [P, D], F32))

        def sem(name):
            return ctx.enter_context(nc.semaphore(name))

        names = ["W0", "M1", "V1", "Q2", "K2", "V2", "P2", "Q3", "K3", "V3"]
        w_hi = {n: sb(f"{n}_hi", [P, NC, D], F16) for n in names}
        w_lo = {n: sb(f"{n}_lo", [P, NC, D], F16) for n in names}
        x_in = sb("x_in", [P, NT, D], F32)
        x_mid = sb("x_mid", [P, NT, D], F32)
        x_late = sb("x_late", [P, NT, D], F32)
        work = sb("work", [P, NT, D], F32)
        h_b = sb("h_b", [P, 2, D], F32)
        h_a = sb("h_a", [P, 2, D], F32)
        ht_b_hi, ht_b_lo = (sb(f"ht_b_{s}", [P, NC, ROWS], F16) for s in ("hi", "lo"))
        ht_a_hi, ht_a_lo = (sb(f"ht_a_{s}", [P, NC, ROWS], F16) for s in ("hi", "lo"))
        q_hi, q_lo = (sb(f"q_{s}", [P, NJ, NT * B2, P], F16) for s in ("hi", "lo"))
        k_hi, k_lo = (sb(f"k_{s}", [P, NC, ROWS], F16) for s in ("hi", "lo"))
        qb_hi, qb_lo = k_hi, k_lo
        vb_hi, vb_lo = (sb(f"vb_{s}", [P, NT, D], F16) for s in ("hi", "lo"))
        v_nat = sb("v_nat", [P, NT, 2, D], F16)
        pt_hi, pt_lo = (sb(f"pt_{s}", [P, 2, H, P], F16) for s in ("hi", "lo"))
        rel = sb("rel", [P, NT, P], F32)
        rel_sq = sb("rel_sq", [P, NT, P], F32)
        rel_hi, rel_lo = (sb(f"rel_{s}", [P, NT, P], F16) for s in ("hi", "lo"))
        bias0, biasp, gamma, beta, biasv = (sb(n, [P, D], F32) for n in ("bias0", "biasp", "gamma", "beta", "biasv"))
        bias_q, bias_k = sb("bias_q", [P, NC], F32), sb("bias_k", [P, NC], F32)
        ident = sb("ident", [P, P], F32)
        adj_row = sb("adj_row", [P, N], F32)
        adj_bd = sb("adj_bd", [P, P], F32)
        adj_sc = sb("adj_sc", [P, P], F32)
        adj_norm_t = sb("adj_norm_t", [P, P], F32)
        mask2, mask3 = sb("mask2", [P, N], F32), sb("mask3", [P, N], F32)
        ones = sb("ones", [P, 1], F32)
        neg_half = sb("neg_half", [P, 1], F32)
        deg = sb("deg", [P, 4], F32)
        NL = 5
        bn6 = sb("bn6", [P, NL, NT, 6], F32)
        mean_var = sb("mean_var", [P, NL, NT, 2], F32)
        var_eps = sb("var_eps", [P, NL, NT], F32)
        rstd = sb("rstd", [P, NL, NT], F32)
        nbias = sb("nbias", [P, NL, NT], F32)
        row_max = sb("row_max", [P, NT, H], F32)
        row_sum = sb("row_sum", [P, NT, H], F32)
        row_inv = sb("row_inv", [P, NT, H], F32)
        rel_ssq = sb("rel_ssq", [P, NT], F32)
        rel_rn = sb("rel_rn", [P, NT], F32)

        bank_w = [bank("bank_w0"), bank("bank_w1")]
        bank_s = [bank("bank_s0"), bank("bank_s1")]
        bank_p = [bank("bank_p0"), bank("bank_p1")]
        bank_b = [bank("bank_b0"), bank("bank_b1")]

        NB, NPJ, NW, NS = 26, 28, 24, 8
        NB_HI, NP_HI, NW_HI = 16, 24, 20
        J_ADJ, J_PROJ0, J_T1, J_M1 = 0, 4, 8, 12
        J_REL, J_SSQ, J_V1, J_OUT1 = 17, 19, (16, 18, 20, 21), 22
        J_Q = {2: 0, 3: 16}
        J_K = {2: 4, 3: 20}
        J_V = {2: 8, 3: 24}
        J_PR2 = 12
        HI_Q, HI_K, HI_V = {2: 0, 3: 12}, {2: 4, 3: 16}, {2: 8, 3: 20}
        PV_ORDER = [("pt", 0), ("pt", 1), ("pv", 0), ("pt", 2), ("pv", 1), ("pt", 3), ("pv", 2), ("pv", 3)]
        J_PT, J_PV = ([PV_ORDER.index((what, t)) for t in range(NT)] for what in ("pt", "pv"))
        J_S = {2: 0, 3: 4}

        def is_group(g, number):
            return isinstance(g, int) and g == number

        def w_turned(L, g):
            if L == 3:
                return NW * g + 12
            return 0 if is_group(g, 0) else NW * g - 8

        def w_attended(L, g):
            return NW * g + (4 if L == 2 else 16 if is_group(g, GROUPS - 1) else 20)

        def w_turned_hi(L, g):
            if L == 3:
                return NW_HI * g + 12
            return 0 if is_group(g, 0) else NW_HI * g - 4

        def w_attended_hi(L, g):
            return NW_HI * g + (4 if L == 2 else 16 if is_group(g, GROUPS - 1) else 20)

        bias0_in, small_in, col_in, adj_in = (sem(n) for n in ("bias0_in", "small_in", "col_in", "adj_in"))
        stage_in = [sem(f"stage_in{i}") for i in range(3)]
        ident_ready, const_ready, zero_ready = sem("ident_ready"), sem("const_ready"), sem("zero_ready")
        setup_v, setup_p, setup_pe = sem("setup_v"), sem("setup_p"), sem("setup_pe")
        conv_hi, conv_lo = sem("conv_hi"), sem("conv_lo")
        adjt_done, blocks_zero = sem("adjt_done"), sem("blocks_zero")
        x_loaded, y_stored = ([sem(f"{n}{t}") for t in range(NT)] for n in ("x_loaded", "y_stored"))
        passed_v, passed_p = sem("passed_v"), sem("passed_p")
        b_done, b_hi, b_lo = sem("b_done"), sem("b_hi"), sem("b_lo")
        p_done, p_hi, p_lo = sem("p_done"), sem("p_hi"), sem("p_lo")
        w_done, w_hi_s, w_lo_s = sem("w_done"), sem("w_hi_s"), sem("w_lo_s")
        s_done, s_read = sem("s_done"), sem("s_read")
        stats_done = [sem(f"stats_done{i}") for i in range(NL)]
        mv_ready = [sem(f"mv_ready{i}") for i in range(NL)]
        ve_ready = [sem(f"ve_ready{i}") for i in range(NL)]
        rstd_ready = [sem(f"rstd_ready{i}") for i in range(NL)]
        nbias_ready = [sem(f"nbias_ready{i}") for i in range(4)]
        h_ready = [sem(f"h_ready{i}") for i in range(4)]
        xb0_ready = sem("xb0_ready")
        sq_ready, relhi_ready, rello_ready = sem("sq_ready"), sem("relhi_ready"), sem("rello_ready")
        rn_ready = sem("rn_ready")
        max_ready = {L: sem(f"max_ready{L}") for L in (2, 3)}
        sub_ready = {L: sem(f"sub_ready{L}") for L in (2, 3)}
        exp_ready = {L: sem(f"exp_ready{L}") for L in (2, 3)}
        sum_ready = {L: sem(f"sum_ready{L}") for L in (2, 3)}
        inv_ready = {L: sem(f"inv_ready{L}") for L in (2, 3)}
        prob_ready = sem("prob_ready")
        xbeta_ready, xo_ready, og_ready, x3_ready, xb3_ready = (
            sem(n) for n in ("xbeta_ready", "xo_ready", "og_ready", "x3_ready", "xb3_ready"))

        stage = [x_mid, x_late, work]
        loads = [("W0", w0, 0), ("wq", wq1, 1), ("wk", wk1, 2), ("wv", wv1, 0),
                 ("Q2", wqkv2[:, 0:D], 1), ("K2", wqkv2[:, D:2 * D], 2), ("V2", wqkv2[:, 2 * D:3 * D], 0),
                 ("P2", wp2, 1), ("Q3", wq3, 2), ("K3", wk3, 1), ("V3", wv3, 2)]
        slot_turn = {}
        for n, (name, _, slot) in enumerate(loads):
            slot_turn[name] = sum(1 for m in loads[:n + 1] if m[2] == slot)
        converted = [n for n, _, _ in loads if n[0] in "WQKVP"]

        conv_count = {n: k + 1 + (2 * NC if k else 0) for k, n in enumerate(converted)}

        C_M1, C_V1 = 1, 1 + NC
        CONVERSIONS = len(converted) + 2 * NC
        prod = [bank_w[0], bank_w[1], bank_s[0], bank_s[1]]
        turned = [bank_p[0], bank_p[1], bank_w[0], bank_w[1]]

        block = ctx.enter_context(nc.Block())

        @block.sync
        def _(sp):
            for b in range(B2):
                sp.dma_start(adj_row[b * N:(b + 1) * N, :], adj).then_inc(adj_in, 16)

            def load_rows(g):
                for t in range(NT):
                    if counts(NB * (g - 1) + J_OUT1 + t + 1):
                        sp.wait_ge(b_lo, NB * (g - 1) + J_OUT1 + t + 1)
                    sp.dma_start(x_in[:, t, :], x_rows[bass.ds(g * ROWS + t * P, P), :]).then_inc(x_loaded[t], 16)

            def store_rows(g):
                for t in range(NT):
                    sp.wait_ge(w_lo_s, w_attended(3, g) + J_PV[t] + 1)
                    sp.dma_start(y_rows[bass.ds(g * ROWS + t * P, P), :], x_late[:, t, :]).then_inc(y_stored[t], 16)

            load_rows(0)
            for n, (name, src, slot) in enumerate(loads):
                if n >= 3:
                    before = [m[0] for m in loads[:n] if m[2] == slot][-1]
                    if before in converted:
                        sp.wait_ge(conv_lo, conv_count[before])
                    else:
                        sp.wait_ge(setup_pe, {"wq": NC, "wk": NC, "wv": NC + 1}[before])
                sp.dma_start(stage[slot][:, :, :], src.rearrange("(c p) n -> p c n", p=P)).then_inc(stage_in[slot], 16)
                if n == 0:
                    sp.dma_start(bias0[:, :], b0.partition_broadcast(P)).then_inc(bias0_in, 16)
                if n == 2:
                    for dst, src1 in ((biasp, bp2), (gamma, gam2), (beta, bet2), (biasv, bv3)):
                        sp.dma_start(dst[:, :], src1.partition_broadcast(P)).then_inc(small_in, 16)
                    for dst, src1 in ((bias_q, bq3), (bias_k, bk3)):
                        sp.dma_start(dst[:, :], src1.rearrange("(c p) -> p c", p=P),
                                     allow_slow_non_contiguous=True).then_inc(col_in, 16)

            load_rows(1)
            with sp.Fori(2, GROUPS) as i:
                load_rows(i)
                store_rows(i - 2)
            store_rows(GROUPS - 2)
            store_rows(GROUPS - 1)
            for t in range(NT):
                sp.wait_ge(y_stored[t], 16 * GROUPS)

        @block.tensor
        def _(pe):
            def passes(dst, pairs):
                n = 0
                for lhs, rhs in pairs:
                    for a, b in ((0, 0), (0, 1), (1, 0)):
                        mm = pe.matmul(dst, lhs[a], rhs[b], start=(n == 0),
                                       stop=(n == 3 * len(pairs) - 1))
                        n += 1
                return mm

            pe.wait_ge(ident_ready, 1)
            pe.wait_ge(setup_v, 6)
            pe.transpose(bank_w[0][:, 0:P], adj_sc[:, :], ident[:, :]).then_inc(adjt_done, 1)
            pe.wait_ge(setup_v, 7)

            def conv_w0():
                pe.wait_ge(conv_lo, 1)

            def multiply_m1(fc):
                if fc == 0:
                    pe.wait_ge(stage_in[1], 16)
                    pe.wait_ge(stage_in[2], 16)
                for ec in range(NC):
                    mm = pe.matmul(prod[fc][:, :], x_late[:, ec, fc * P:(fc + 1) * P], work[:, ec, :],
                                   start=(ec == 0), stop=(ec == NC - 1))
                mm.then_inc(setup_pe, 1)

            def conv_m1():
                pe.wait_ge(conv_lo, C_M1 + NC)

            def turn_v1():
                pe.wait_ge(stage_in[0], 32)
                pe.wait_ge(conv_lo, C_M1 + 2)
                for dc in range(NC):
                    for ec in range(NC):
                        mm = pe.transpose(turned[dc][:, ec * P:(ec + 1) * P], x_mid[:, ec, dc * P:(dc + 1) * P],
                                          ident[:, :])
                mm.then_inc(setup_pe, 1)

            def conv_v1():
                pe.wait_ge(conv_lo, C_V1 + NC)

            def set_up_done():
                pe.wait_ge(conv_lo, conv_count["Q3"])

            def conv_all():
                pe.wait_ge(conv_lo, CONVERSIONS)

            def b_bank(g, j):
                if counts(NB * g + j - 1):
                    pe.wait_ge(b_lo, NB * g + j - 1)
                return bank_b[j % 2]

            def adj0(g, t):
                dst = b_bank(g, J_ADJ + t)
                pe.wait_ge(h_ready[0], 4 * g + t + 1)
                for c in range(NC):
                    mm = pe.matmul(dst[:, c * P:(c + 1) * P], h_b[:, t % 2, c * P:(c + 1) * P], adj_norm_t[:, :],
                                   start=(c == 0), stop=(c == NC - 1), skip_group_check=True)
                mm.then_inc(b_done, 1)

            def rows_product(dst, w, ht, t):
                return passes(dst[:, :], [((ht[0][:, c, t * P:(t + 1) * P], ht[1][:, c, t * P:(t + 1) * P]),
                                           (w_hi[w][:, c, :], w_lo[w][:, c, :])) for c in range(NC)])

            def cols_product(dst, w, ht, oc):
                s = slice(oc * P, (oc + 1) * P)
                return passes(dst[:, :], [((w_hi[w][:, c, s], w_lo[w][:, c, s]),
                                           (ht[0][:, c, :], ht[1][:, c, :])) for c in range(NC)])

            HT_B, HT_A = (ht_b_hi, ht_b_lo), (ht_a_hi, ht_a_lo)

            def proj0(g, t):
                dst = b_bank(g, J_PROJ0 + t)
                pe.wait_ge(b_lo, NB * g + J_ADJ + t + 1)
                rows_product(dst, "W0", HT_B, t).then_inc(b_done, 1)

            def turn1(g, t):
                dst = b_bank(g, J_T1 + t)
                pe.wait_ge(h_ready[1], 4 * g + t + 1)
                for c in range(NC):
                    mm = pe.transpose(dst[:, c * P:(c + 1) * P], h_b[:, t % 2, c * P:(c + 1) * P], ident[:, :])
                mm.then_inc(b_done, 1)

            def query1(g, c):
                dst = b_bank(g, J_M1 + c)
                if c == 0:
                    pe.wait_ge(b_lo, NB * g + J_T1 + NT)
                cols_product(dst, "M1", HT_B, c).then_inc(b_done, 1)

            def relation1(g):
                dst = b_bank(g, J_REL)
                pe.wait_ge(b_lo, NB * g + J_M1 + NC)
                n = 0
                for t in range(NT):
                    s = slice(t * P, (t + 1) * P)
                    for c in range(NC):
                        for k, q in ((ht_b_hi, qb_hi), (ht_b_hi, qb_lo), (ht_b_lo, qb_hi)):
                            mm = pe.matmul(dst[:, s], k[:, c, s], q[:, c, s], start=(n == 0),
                                           stop=(n == 3 * NC * NT - 1), skip_group_check=True)
                            n += 1
                mm.then_inc(b_done, 1)

            def square_sum1(g):
                dst = b_bank(g, J_SSQ)
                pe.wait_ge(sq_ready, g + 1)
                for t in range(NT):
                    mm = pe.matmul(dst[:, t:t + 1], rel_sq[:, t, :], ones[:, :], start=(t == 0),
                                   stop=(t == NT - 1), skip_group_check=True)
                mm.then_inc(b_done, 1)

            def value1(g, t):
                rows_product(b_bank(g, J_V1[t]), "V1", HT_B, t).then_inc(b_done, 1)

            def out1(g, t):
                dst = b_bank(g, J_OUT1 + t)
                pe.wait_ge(rello_ready, g + 1)
                pe.wait_ge(b_lo, NB * g + J_V1[t] + 1)
                passes(dst[:, :], [((rel_hi[:, t, :], rel_lo[:, t, :]),
                                    (vb_hi[:, t, :], vb_lo[:, t, :]))]).then_inc(b_done, 1)

            def w_bank(job, t):
                if counts(job - 1):
                    pe.wait_ge(w_lo_s, job - 1)
                return bank_w[t % 2]

            def p_bank(g, j):
                if counts(NPJ * g + j - 1):
                    pe.wait_ge(p_lo, NPJ * g + j - 1)
                return bank_p[j % 2]

            def turn(L, g, t):
                dst = w_bank(w_turned(L, g) + t, t)
                pe.wait_ge(h_ready[L], 4 * g + t + 1)
                for c in range(NC):
                    mm = pe.transpose(dst[:, c * P:(c + 1) * P], h_a[:, t % 2, c * P:(c + 1) * P], ident[:, :])
                mm.then_inc(w_done, 1)

            def query(L, g, c):
                dst = p_bank(g, J_Q[L] + c)
                if c == 0:
                    pe.wait_ge(w_lo_s, w_turned(L, g) + NT)
                cols_product(dst, f"Q{L}", HT_A, c).then_inc(p_done, 1)

            def key(L, g, c):
                cols_product(p_bank(g, J_K[L] + c), f"K{L}", HT_A, c).then_inc(p_done, 1)

            def value(L, g, t):
                rows_product(p_bank(g, J_V[L] + t), f"V{L}", HT_A, t).then_inc(p_done, 1)

            def scores(L, g, t):
                job = NS * g + J_S[L] + t
                if counts(job - 1):
                    pe.wait_ge(s_read, job - 1)
                if t == 0:
                    pe.wait_ge(p_lo, NPJ * g + J_K[L] + NC)
                for j in range(NJ):
                    for b in range(B2):
                        dst = bank_s[t % 2][:, (j * B2 + b) * N:(j * B2 + b + 1) * N]
                        keys = slice(t * P + b * N, t * P + (b + 1) * N)
                        for n, (q, k) in enumerate(((q_hi, k_hi), (q_hi, k_lo), (q_lo, k_hi))):
                            mm = pe.matmul(dst, q[:, j, t * B2 + b, :], k[:, j, keys],
                                           start=(j == 0 and b == 0 and n == 0), stop=(n == 2), skip_group_check=True)
                mm.then_inc(s_done, 1)

            def turn_weights(L, g, t):
                dst = w_bank(w_attended(L, g) + J_PT[t], J_PT[t])
                pe.wait_ge(prob_ready, 8 * g + (4 if L == 3 else 0) + t + 1)
                for j in range(NJ):
                    mm = pe.transpose(dst[:, j * P:(j + 1) * P], work[:, t, j * P:(j + 1) * P], ident[:, :])
                mm.then_inc(w_done, 1)

            def attend(L, g, t):
                dst = w_bank(w_attended(L, g) + J_PV[t], J_PV[t])
                pe.wait_ge(w_lo_s, w_attended(L, g) + J_PT[t] + 1)
                pe.wait_ge(p_lo, NPJ * g + J_V[L] + t + 1)
                for h in range(H):
                    j, r = h // 2, h % 2
                    v = [v_nat[:, t, s, h * HD:(h + 1) * HD] for s in range(2)]
                    p = [pt[:, t % 2, h, :] for pt in (pt_hi, pt_lo)]
                    for n, (sv, sp_) in enumerate(((0, 0), (0, 1), (1, 0))):
                        if L == 2:
                            mm = pe.matmul(dst[r * HD:(r + 1) * HD, j * P:(j + 1) * P], v[sv], p[sp_],
                                           start=(j == 0 and n == 0), stop=(n == 2), skip_group_check=True)
                        else:
                            mm = pe.matmul(dst[:, h * HD:(h + 1) * HD], p[sp_], v[sv],
                                           start=(h == 0 and n == 0), stop=(n == 2), skip_group_check=True)
                mm.then_inc(w_done, 1)

            def project2(g, t):
                dst = p_bank(g, J_PR2 + t)
                pe.wait_ge(w_lo_s, w_attended(2, g) + J_PV[t] + 1)
                rows_product(dst, "P2", HT_A, t).then_inc(p_done, 1)

            def body(gb, ga, gp):
                a, b, p = ga is not None, gb is not None, gp is not None
                first, second = is_group(gb, 0), is_group(ga, 0)
                for t in range(2):
                    if a:
                        query(2, ga, t)
                    if p:
                        attend(3, gp, t)
                        turn_weights(3, gp, t + 2)
                for t in range(2, 4):
                    if a:
                        query(2, ga, t)
                    if p:
                        attend(3, gp, t)
                for t in range(NT):
                    if a:
                        key(2, ga, t)
                    if b:
                        adj0(gb, t)
                if first:
                    conv_w0()
                if b:
                    proj0(gb, 0)
                if a:
                    scores(2, ga, 0)
                    scores(2, ga, 1)
                    value(2, ga, 0)
                if b:
                    proj0(gb, 1)
                if a:
                    for t in range(2, 4):
                        scores(2, ga, t)
                        value(2, ga, t - 1)
                    value(2, ga, 3)
                    turn_weights(2, ga, 0)
                for t in range(1, 3):
                    if a:
                        turn_weights(2, ga, t)
                    if b:
                        proj0(gb, t + 1)
                    if a:
                        attend(2, ga, t - 1)
                if a:
                    turn_weights(2, ga, 3)
                if b:
                    turn1(gb, 0)
                if a:
                    project2(ga, 0)
                    attend(2, ga, 2)
                if b:
                    turn1(gb, 1)
                if first:
                    multiply_m1(0)
                if a:
                    project2(ga, 1)
                    attend(2, ga, 3)
                if first:
                    multiply_m1(1)
                if b:
                    turn1(gb, 2)
                if a:
                    project2(ga, 2)
                if b:
                    turn1(gb, 3)
                if first:
                    multiply_m1(2)
                    multiply_m1(3)
                if a:
                    project2(ga, 3)
                if first:
                    turn_v1()
                    conv_m1()
                if b:
                    for t in range(3):
                        query1(gb, t)
                if a:
                    turn(3, ga, 0)
                if b:
                    query1(gb, 3)
                if a:
                    turn(3, ga, 1)
                if first:
                    conv_v1()
                if b:
                    value1(gb, 0)
                if a:
                    turn(3, ga, 2)
                if b:
                    relation1(gb)
                if a:
                    turn(3, ga, 3)
                if b:
                    value1(gb, 1)
                    square_sum1(gb)
                if second:
                    conv_all()
                for t in range(2):
                    if a:
                        query(3, ga, t)
                    if b:
                        value1(gb, t + 2)
                for t in range(2, 4):
                    if a:
                        query(3, ga, t)
                    if b:
                        out1(gb, t - 2)
                for t in range(2):
                    if a:
                        key(3, ga, t)
                    if b:
                        out1(gb, t + 2)
                if a:
                    key(3, ga, 2)
                    key(3, ga, 3)
                    value(3, ga, 0)
                    scores(3, ga, 0)
                for t in range(1, 4):
                    if a:
                        scores(3, ga, t)
                        value(3, ga, t)
                    if b:
                        turn(2, gb, t - 1)
                if b:
                    turn(2, gb, 3)
                if a:
                    turn_weights(3, ga, 0)
                    turn_weights(3, ga, 1)
                if first:
                    set_up_done()

            body(0, None, None)
            body(1, 0, None)
            with pe.Fori(2, GROUPS) as i:
                body(i, i - 1, i - 2)
            body(None, GROUPS - 1, GROUPS - 2)
            body(None, None, GROUPS - 1)

        @block.scalar
        def _(act):
            def hi_weights(name):
                slot = {n: s for n, _, s in loads}[name]
                act.wait_ge(stage_in[slot], 16 * slot_turn[name])
                act.activation(w_hi[name][:, :, :], stage[slot][:, :, :], ACT.Copy, scale=WS).then_inc(conv_hi, 1)

            def conv_w0():
                hi_weights("W0")

            def conv_m1(c):
                act.wait_ge(setup_pe, c + 1)
                act.activation(w_hi["M1"][:, c, :], prod[c][:, :], ACT.Copy, scale=WS).then_inc(conv_hi, 1)

            def conv_v1():
                act.wait_ge(setup_pe, NC + 1)
                for c in range(NC):
                    act.activation(w_hi["V1"][:, c, :], turned[c][:, :], ACT.Copy, scale=WS).then_inc(conv_hi, 1)

            others = iter(converted[1:])

            def conv_next():
                hi_weights(next(others))

            def set_up_done():
                act.wait_ge(setup_v, 11)
                act.wait_ge(blocks_zero, 1)

            def relu(L, src, h, t, g, free_sem, free_at):
                act.wait_ge(nbias_ready[L], 4 * g + t + 1)
                if counts(free_at):
                    act.wait_ge(free_sem, free_at)
                act.activation(h[:, t % 2, :], src[:, t, :], ACT.Relu, bias=nbias[:, L, t:t + 1],
                               scale=rstd[:, L, t:t + 1]).then_inc(h_ready[L], 1)

            def relu0(g, t):
                relu(0, x_in, h_b, t, g, b_done, NB * g + (J_T1 + t + 3 - NB if t < 2 else J_ADJ + t - 1))

            def relu1(g, t):
                relu(1, x_in, h_b, t, g, b_done, NB * g + (J_ADJ + t + 3 if t < 2 else J_T1 + t - 1))

            def relu2(g, t):
                relu(2, x_mid, h_a, t, g, w_done, w_turned(3, g - 1) + t + 3 if t < 2 else w_turned(2, g) + t - 1)

            def relu3(g, t):
                relu(3, x_late, h_a, t, g, w_done, w_turned(2, g) + t + 3 if t < 2 else w_turned(3, g) + t - 1)

            def tile_cols(buf, t):
                return buf[:, :, t * P:(t + 1) * P]

            def chunks(bank):
                return bank[:, :].rearrange("p (c r) -> p c r", c=NC)

            def b_read(g, j, dst, shaped=False, **kw):
                act.wait_ge(b_done, NB * g + j + 1)
                src = bank_b[j % 2]
                act.activation(dst, chunks(src) if shaped else src[:, :], ACT.Copy, **kw).then_inc(b_hi, 1)

            def adj0_hi(g, t):
                b_read(g, J_ADJ + t, tile_cols(ht_b_hi, t), True)

            def turn1_hi(g, t):
                b_read(g, J_T1 + t, tile_cols(ht_b_hi, t), True)

            def query1_hi(g, c):
                b_read(g, J_M1 + c, qb_hi[:, c, :])

            def value1_hi(g, t):
                b_read(g, J_V1[t], vb_hi[:, t, :])

            def relation1_hi(g):
                act.wait_ge(b_lo, NB * g + J_REL + 1)
                act.activation(rel_sq[:, :, :], rel[:, :, :], ACT.Square).then_inc(sq_ready, 1)
                act.activation(rel_hi[:, :, :], rel[:, :, :], ACT.Copy).then_inc(relhi_ready, 1)

            def turn_hi(L, g, t):
                act.wait_ge(w_done, w_turned(L, g) + t + 1)
                act.activation(tile_cols(ht_a_hi, t), chunks(bank_w[t % 2]), ACT.Copy).then_inc(w_hi_s, 1)

            def query_hi(L, g, c):
                j = J_Q[L] + c
                act.wait_ge(p_done, NPJ * g + j + 1)
                for r in range(2):
                    f = slice(r * HD, (r + 1) * HD)
                    dst = q_hi[f, c, :, r * N:(r + 1) * N]
                    src = bank_p[j % 2][f, :].rearrange("p (g q) -> p g q", q=N)
                    if L == 3:
                        cp = act.activation(dst, src, ACT.Identity, bias=bias_q[f, c:c + 1])
                    else:
                        cp = act.activation(dst, src, ACT.Copy)
                cp.then_inc(p_hi, 1)

            def key_hi(L, g, c):
                j = J_K[L] + c
                act.wait_ge(p_done, NPJ * g + j + 1)
                if L == 3:
                    act.activation(k_hi[:, c, :], bank_p[j % 2][:, :], ACT.Identity, bias=bias_k[:, c:c + 1])\
                       .then_inc(p_hi, 1)
                else:
                    act.activation(k_hi[:, c, :], bank_p[j % 2][:, :], ACT.Copy).then_inc(p_hi, 1)

            def value_hi(L, g, t):
                j = J_V[L] + t
                act.wait_ge(p_done, NPJ * g + j + 1)
                act.activation(v_nat[:, t, 0, :], bank_p[j % 2][:, :], ACT.Copy).then_inc(p_hi, 1)

            def exp(L, g, t):
                act.wait_ge(sub_ready[L], 4 * g + t + 1)
                act.activation(work[:, t, :], work[:, t, :], ACT.Exp, scale=SCALE / (WS * WS)).then_inc(exp_ready[L], 1)

            def weights_hi(L, g, t):
                act.wait_ge(w_done, w_attended(L, g) + J_PT[t] + 1)
                for b in range(B2):
                    k = slice(b * N, (b + 1) * N)
                    src = bank_w[J_PT[t] % 2][k, :].rearrange("p (h q) -> p h q", h=H)
                    cp = act.activation(pt_hi[k, t % 2, :, k], src, ACT.Copy, scale=PS)
                cp.then_inc(w_hi_s, 1)

            def attn2_hi(g, t):
                act.wait_ge(w_done, w_attended(2, g) + J_PV[t] + 1)
                act.activation(tile_cols(ht_a_hi, t), chunks(bank_w[J_PV[t] % 2]), ACT.Copy, scale=1.0 / PS)\
                   .then_inc(w_hi_s, 1)

            def body(gb, ga, gp):
                a, b, p = ga is not None, gb is not None, gp is not None
                first, second = is_group(gb, 0), is_group(ga, 0)
                for t in range(2):
                    if a:
                        query_hi(2, ga, t)
                    if p:
                        weights_hi(3, gp, t + 2)
                for t in range(2):
                    if b:
                        relu0(gb, t)
                    if a:
                        query_hi(2, ga, t + 2)
                if first:
                    conv_w0()
                if a:
                    key_hi(2, ga, 0)
                if b:
                    adj0_hi(gb, 0)
                    relu0(gb, 2)
                if a:
                    key_hi(2, ga, 1)
                if second:
                    conv_next()
                if b:
                    adj0_hi(gb, 1)
                    relu0(gb, 3)
                if second:
                    conv_next()
                for t in range(2, 4):
                    if a:
                        key_hi(2, ga, t)
                    if b:
                        adj0_hi(gb, t)
                for t in range(2):
                    if a:
                        exp(2, ga, t)
                        value_hi(2, ga, t)
                    if b:
                        relu1(gb, t)
                if a:
                    for t in range(2, 4):
                        exp(2, ga, t)
                        value_hi(2, ga, t)
                    weights_hi(2, ga, 0)
                    for t in range(1, 3):
                        weights_hi(2, ga, t)
                        attn2_hi(ga, t - 1)
                    weights_hi(2, ga, 3)
                if b:
                    turn1_hi(gb, 0)
                    relu1(gb, 2)
                if a:
                    attn2_hi(ga, 2)
                if b:
                    turn1_hi(gb, 1)
                    relu1(gb, 3)
                if first:
                    conv_m1(0)
                if a:
                    attn2_hi(ga, 3)
                if first:
                    conv_m1(1)
                if b:
                    turn1_hi(gb, 2)
                    turn1_hi(gb, 3)
                if first:
                    conv_m1(2)
                    conv_m1(3)
                    conv_v1()
                if b:
                    query1_hi(gb, 0)
                if a:
                    relu3(ga, 0)
                if b:
                    query1_hi(gb, 1)
                if first:
                    conv_next()
                if a:
                    relu3(ga, 1)
                if b:
                    query1_hi(gb, 2)
                if first:
                    conv_next()
                if a:
                    turn_hi(3, ga, 0)
                    relu3(ga, 2)
                if b:
                    query1_hi(gb, 3)
                if a:
                    turn_hi(3, ga, 1)
                    relu3(ga, 3)
                if b:
                    value1_hi(gb, 0)
                if first:
                    conv_next()
                if a:
                    turn_hi(3, ga, 2)
                if b:
                    relation1_hi(gb)
                if a:
                    turn_hi(3, ga, 3)
                if b:
                    value1_hi(gb, 1)
                if first:
                    conv_next()
                if a:
                    query_hi(3, ga, 0)
                if b:
                    value1_hi(gb, 2)
                if first:
                    conv_next()
                if a:
                    query_hi(3, ga, 1)
                if b:
                    value1_hi(gb, 3)
                if a:
                    query_hi(3, ga, 2)
                    query_hi(3, ga, 3)
                for t in range(2):
                    if a:
                        key_hi(3, ga, t)
                    if b:
                        relu2(gb, t)
                if a:
                    key_hi(3, ga, 2)
                    key_hi(3, ga, 3)
                    value_hi(3, ga, 0)
                for t in range(2):
                    if a:
                        exp(3, ga, t)
                        value_hi(3, ga, t + 1)
                    if b:
                        turn_hi(2, gb, t)
                        relu2(gb, t + 2)
                if a:
                    exp(3, ga, 2)
                    value_hi(3, ga, 3)
                if b:
                    turn_hi(2, gb, 2)
                    turn_hi(2, gb, 3)
                if a:
                    exp(3, ga, 3)
                    weights_hi(3, ga, 0)
                    weights_hi(3, ga, 1)
                if first:
                    set_up_done()

            body(0, None, None)
            body(1, 0, None)
            with act.Fori(2, GROUPS) as i:
                body(i, i - 1, i - 2)
            body(None, GROUPS - 1, GROUPS - 2)
            body(None, None, GROUPS - 1)

        @block.vector
        def _(dve):
            dve.wait_ge(adj_in, 16 * B2)
            dve.tensor_reduce(deg[:, 0:1], adj_row[:, :], AX.X, ALU.add).then_inc(setup_v, 1)
            dve.wait_ge(const_ready, 1)
            for b in range(B2):
                dve.tensor_copy(adj_bd[b * N:(b + 1) * N, b * N:(b + 1) * N], adj_row[b * N:(b + 1) * N, :])\
                   .then_inc(setup_v, 1)
            dve.wait_ge(setup_v, 3)
            dve.tensor_scalar(deg[:, 1:2], deg[:, 0:1], TINY, None, ALU.max).then_inc(setup_v, 1)
            dve.tensor_scalar(deg[:, 2:3], deg[:, 0:1], 0.0, None, ALU.is_gt).then_inc(setup_v, 1)
            dve.wait_ge(setup_v, 5)
            dve.wait_ge(setup_p, 1)
            dve.tensor_scalar(adj_sc[:, :], adj_bd[:, :], deg[:, 3:4], deg[:, 2:3], ALU.mult, ALU.mult)\
               .then_inc(setup_v, 1)
            dve.wait_ge(adjt_done, 1)
            dve.tensor_scalar(adj_norm_t[:, :], bank_w[0][:, 0:P], deg[:, 3:4], deg[:, 2:3], ALU.mult, ALU.mult)\
               .then_inc(setup_v, 1)
            dve.tensor_scalar(mask2[:, :], adj_row[:, :], 0.0, -3e38, ALU.is_equal, ALU.mult).then_inc(setup_v, 1)
            dve.tensor_scalar(mask3[:, :], adj_row[:, :], 0.0, -1e9 / SCALE * WS * WS, ALU.is_equal, ALU.mult)\
               .then_inc(setup_v, 1)

            slots = {n: s for n, _, s in loads}

            def lo_weights(n, dst, src, hi):
                dve.wait_ge(conv_hi, n)
                dve.scalar_tensor_tensor(out=dst, in0=src, scalar=WS, in1=hi, op0=ALU.mult, op1=ALU.subtract)\
                   .then_inc(conv_lo, 1)

            def lo_flat(name):
                lo_weights(conv_count[name], w_lo[name][:, :, :], stage[slots[name]][:, :, :], w_hi[name][:, :, :])

            def conv_w0():
                lo_flat("W0")

            def conv_m1(c):
                lo_weights(C_M1 + c + 1, w_lo["M1"][:, c, :], prod[c][:, :], w_hi["M1"][:, c, :])

            def conv_v1():
                for c in range(NC):
                    lo_weights(C_V1 + c + 1, w_lo["V1"][:, c, :], turned[c][:, :], w_hi["V1"][:, c, :])

            others = iter(converted[1:])

            def conv_next():
                lo_flat(next(others))

            def set_up_done():
                dve.wait_ge(col_in, 32)
                dve.tensor_scalar(bias_q[:, :], bias_q[:, :], WS, None, ALU.mult).then_inc(setup_v, 1)
                dve.tensor_scalar(bias_k[:, :], bias_k[:, :], WS, None, ALU.mult).then_inc(setup_v, 1)
                dve.wait_ge(setup_v, 11)
                dve.wait_ge(small_in, 16 * 4)
                dve.wait_ge(blocks_zero, 1)

            def stats(L, src, g, t):
                dve.bn_stats(bn6[:, L, t, :], src[:, t, :]).then_inc(stats_done[L], 1)
                dve.wait_ge(stats_done[L], 4 * g + t + 1)
                dve.sem_inc(passed_v, 1)
                dve.bn_aggr(mean_var[:, L, t, :], bn6[:, L, t, :]).then_inc(mv_ready[L], 1)

            def tile_cols(buf, t):
                return buf[:, :, t * P:(t + 1) * P]

            def chunks(bank):
                return bank[:, :].rearrange("p (c r) -> p c r", c=NC)

            def lo(dst, src, hi, sem_, scale=None):
                if scale is None:
                    dve.tensor_tensor(dst, src, hi, ALU.subtract).then_inc(sem_, 1)
                else:
                    dve.scalar_tensor_tensor(out=dst, in0=src, scalar=scale, in1=hi, op0=ALU.mult,
                                             op1=ALU.subtract).then_inc(sem_, 1)

            def norm0(g, t):
                dve.wait_ge(x_loaded[t], 16 * g + 16)
                stats(0, x_in, g, t)

            def adj0_lo(g, t):
                dve.wait_ge(b_hi, NB_HI * g + t + 1)
                lo(tile_cols(ht_b_lo, t), chunks(bank_b[(J_ADJ + t) % 2]), tile_cols(ht_b_hi, t), b_lo)

            def residual0(g, t):
                dve.wait_ge(b_done, NB * g + J_PROJ0 + t + 1)
                dve.wait_ge(xb0_ready, 4 * g + t + 1)
                dve.scalar_tensor_tensor(out=x_in[:, t, :], in0=bank_b[(J_PROJ0 + t) % 2][:, :], scalar=1.0 / WS,
                                         in1=x_in[:, t, :], op0=ALU.mult, op1=ALU.add).then_inc(b_lo, 1)
                dve.wait_ge(b_lo, NB * g + J_PROJ0 + t + 1)
                stats(1, x_in, g, t)

            def turn1_lo(g, t):
                dve.wait_ge(b_hi, NB_HI * g + 4 + t + 1)
                lo(tile_cols(ht_b_lo, t), chunks(bank_b[(J_T1 + t) % 2]), tile_cols(ht_b_hi, t), b_lo)

            def query1_lo(g, c):
                dve.wait_ge(b_hi, NB_HI * g + 8 + c + 1)
                lo(qb_lo[:, c, :], bank_b[(J_M1 + c) % 2][:, :], qb_hi[:, c, :], b_lo)

            def value1_lo(g, t):
                dve.wait_ge(b_hi, NB_HI * g + 12 + t + 1)
                lo(vb_lo[:, t, :], bank_b[J_V1[t] % 2][:, :], vb_hi[:, t, :], b_lo)

            def relation1(g):
                dve.wait_ge(b_done, NB * g + J_REL + 1)
                dve.scalar_tensor_tensor(out=rel[:, :, :], in0=chunks(bank_b[J_REL % 2]), scalar=1.0 / (WS * WS),
                                         in1=adj_bd[:, :].unsqueeze(1).broadcast_to((P, NT, P)),
                                         op0=ALU.mult, op1=ALU.mult).then_inc(b_lo, 1)

            def relation1_lo(g):
                dve.wait_ge(relhi_ready, g + 1)
                dve.tensor_tensor(rel_lo[:, :, :], rel[:, :, :], rel_hi[:, :, :], ALU.subtract)\
                   .then_inc(rello_ready, 1)

            def ssq1(g):
                dve.wait_ge(b_done, NB * g + J_SSQ + 1)
                dve.tensor_scalar(rel_ssq[:, :], bank_b[J_SSQ % 2][:, 0:NT], WS * WS, None, ALU.mult)\
                   .then_inc(b_lo, 1)

            def residual1(g, t):
                dve.wait_ge(b_done, NB * g + J_OUT1 + t + 1)
                dve.wait_ge(rn_ready, g + 1)
                if counts(4 * g - 3 + t):
                    dve.wait_ge(xo_ready, 4 * g - 3 + t)
                dve.scalar_tensor_tensor(out=x_mid[:, t, :], in0=bank_b[(J_OUT1 + t) % 2][:, :],
                                         scalar=rel_rn[:, t:t + 1], in1=x_in[:, t, :], op0=ALU.mult, op1=ALU.add)\
                   .then_inc(b_lo, 1)
                dve.wait_ge(b_lo, NB * g + J_OUT1 + t + 1)
                stats(2, x_mid, g, t)

            def turn_lo(L, g, t):
                dve.wait_ge(w_hi_s, w_turned_hi(L, g) + t + 1)
                lo(tile_cols(ht_a_lo, t), chunks(bank_w[t % 2]), tile_cols(ht_a_hi, t), w_lo_s)

            def query_lo(L, g, c):
                j = J_Q[L] + c
                dve.wait_ge(p_hi, NP_HI * g + HI_Q[L] + c + 1)
                for r in range(2):
                    f = slice(r * HD, (r + 1) * HD)
                    blocks = (f, c, slice(None), slice(r * N, (r + 1) * N))
                    src = bank_p[j % 2][f, :].rearrange("p (g q) -> p g q", q=N)
                    if L == 3:
                        sub = dve.scalar_tensor_tensor(out=q_lo[blocks], in0=src, scalar=bias_q[f, c:c + 1],
                                                       in1=q_hi[blocks], op0=ALU.add, op1=ALU.subtract)
                    else:
                        sub = dve.tensor_tensor(q_lo[blocks], src, q_hi[blocks], ALU.subtract)
                sub.then_inc(p_lo, 1)

            def key_lo(L, g, c):
                j = J_K[L] + c
                dve.wait_ge(p_hi, NP_HI * g + HI_K[L] + c + 1)
                if L == 3:
                    dve.scalar_tensor_tensor(out=k_lo[:, c, :], in0=bank_p[j % 2][:, :], scalar=bias_k[:, c:c + 1],
                                             in1=k_hi[:, c, :], op0=ALU.add, op1=ALU.subtract).then_inc(p_lo, 1)
                else:
                    lo(k_lo[:, c, :], bank_p[j % 2][:, :], k_hi[:, c, :], p_lo)

            def value_lo(L, g, t):
                j = J_V[L] + t
                dve.wait_ge(p_hi, NP_HI * g + HI_V[L] + t + 1)
                lo(v_nat[:, t, 1, :], bank_p[j % 2][:, :], v_nat[:, t, 0, :], p_lo)

            def per_head(buf, t):
                return buf[:, t, :].rearrange("p (h k) -> p h k", h=H)

            def scores(L, g, t):
                mask = mask2 if L == 2 else mask3
                dve.wait_ge(s_done, NS * g + J_S[L] + t + 1)
                dve.tensor_tensor(per_head(work, t), bank_s[t % 2][:, :].rearrange("p (h k) -> p h k", h=H),
                                  mask[:, :].unsqueeze(1).broadcast_to((P, H, N)), ALU.add).then_inc(s_read, 1)

            def softmax_max(L, g, t):
                dve.wait_ge(s_read, NS * g + J_S[L] + t + 1)
                dve.tensor_reduce(row_max[:, t, :], per_head(work, t), AX.X, ALU.max).then_inc(max_ready[L], 1)

            def softmax_sum(L, g, t):
                dve.wait_ge(exp_ready[L], 4 * g + t + 1)
                dve.tensor_reduce(row_sum[:, t, :], per_head(work, t), AX.X, ALU.add).then_inc(sum_ready[L], 1)
                dve.wait_ge(sum_ready[L], 4 * g + t + 1)
                dve.reciprocal(row_inv[:, t, :], row_sum[:, t, :]).then_inc(inv_ready[L], 1)

            def weights_lo(L, g, t):
                dve.wait_ge(w_hi_s, w_attended_hi(L, g) + (J_PT[t] if L == 2 else t) + 1)
                for b in range(B2):
                    k = slice(b * N, (b + 1) * N)
                    sub = dve.scalar_tensor_tensor(out=pt_lo[k, t % 2, :, k], scalar=PS, in1=pt_hi[k, t % 2, :, k],
                                                   in0=bank_w[J_PT[t] % 2][k, :].rearrange("p (h q) -> p h q", h=H),
                                                   op0=ALU.mult, op1=ALU.subtract)
                sub.then_inc(w_lo_s, 1)

            def attn2_lo(g, t):
                dve.wait_ge(w_hi_s, w_attended_hi(2, g) + J_PV[t] + 1)
                lo(tile_cols(ht_a_lo, t), chunks(bank_w[J_PV[t] % 2]), tile_cols(ht_a_hi, t), w_lo_s, 1.0 / PS)

            def project2(g, t):
                j = J_PR2 + t
                dve.wait_ge(p_done, NPJ * g + j + 1)
                dve.scalar_tensor_tensor(out=work[:, t, :], in0=bank_p[j % 2][:, :], scalar=1.0 / (WS * WS),
                                         in1=biasp[:, :], op0=ALU.mult, op1=ALU.add).then_inc(p_lo, 1)
                dve.wait_ge(p_lo, NPJ * g + j + 1)
                stats(4, work, g, t)

            def residual2(g, t):
                dve.wait_ge(xo_ready, 4 * g + t + 1)
                dve.wait_ge(mv_ready[4], 4 * g + t + 1)
                dve.scalar_tensor_tensor(out=work[:, t, :], in0=work[:, t, :], scalar=mean_var[:, 4, t, 0:1],
                                         in1=gamma[:, :], op0=ALU.subtract, op1=ALU.mult).then_inc(og_ready, 1)
                dve.wait_ge(og_ready, 4 * g + t + 1)
                dve.wait_ge(rstd_ready[4], 4 * g + t + 1)
                dve.scalar_tensor_tensor(out=x_late[:, t, :], in0=work[:, t, :], scalar=rstd[:, 4, t:t + 1],
                                         in1=x_late[:, t, :], op0=ALU.mult, op1=ALU.add).then_inc(x3_ready, 1)
                dve.wait_ge(x3_ready, 4 * g + t + 1)
                stats(3, x_late, g, t)

            def result(g, t):
                job = w_attended(3, g) + J_PV[t] + 1
                dve.wait_ge(w_done, job)
                dve.wait_ge(xb3_ready, 4 * g + t + 1)
                dve.scalar_tensor_tensor(out=x_late[:, t, :], in0=bank_w[J_PV[t] % 2][:, :], scalar=1.0 / (WS * PS),
                                         in1=x_late[:, t, :], op0=ALU.mult, op1=ALU.add).then_inc(w_lo_s, 1)

            def body(gb, ga, gp):
                a, b, p = ga is not None, gb is not None, gp is not None
                first, second = is_group(gb, 0), is_group(ga, 0)
                for t in range(2):
                    if p:
                        result(gp, t)
                    if a:
                        query_lo(2, ga, t)
                    if p:
                        weights_lo(3, gp, t + 2)
                    if b:
                        norm0(gb, t)
                for t in range(2, 4):
                    if p:
                        result(gp, t)
                    if a:
                        query_lo(2, ga, t)
                    if b:
                        norm0(gb, t)
                if first:
                    conv_w0()
                if a:
                    key_lo(2, ga, 0)
                if b:
                    adj0_lo(gb, 0)
                if a:
                    key_lo(2, ga, 1)
                if second:
                    conv_next()
                if b:
                    adj0_lo(gb, 1)
                if a:
                    key_lo(2, ga, 2)
                if second:
                    conv_next()
                if b:
                    adj0_lo(gb, 2)
                if a:
                    key_lo(2, ga, 3)
                if b:
                    adj0_lo(gb, 3)
                    residual0(gb, 0)
                if a:
                    for t in range(2):
                        scores(2, ga, t)
                        softmax_max(2, ga, t)
                    value_lo(2, ga, 0)
                    softmax_sum(2, ga, 0)
                if b:
                    residual0(gb, 1)
                if a:
                    for t in range(2, 4):
                        scores(2, ga, t)
                        softmax_max(2, ga, t)
                        softmax_sum(2, ga, t - 1)
                        value_lo(2, ga, t - 1)
                    softmax_sum(2, ga, 3)
                    value_lo(2, ga, 3)
                    weights_lo(2, ga, 0)
                    weights_lo(2, ga, 1)
                for t in range(2):
                    if a:
                        attn2_lo(ga, t)
                        weights_lo(2, ga, t + 2)
                    if b:
                        residual0(gb, t + 2)
                if b:
                    turn1_lo(gb, 0)
                if a:
                    project2(ga, 0)
                    attn2_lo(ga, 2)
                if b:
                    turn1_lo(gb, 1)
                if first:
                    conv_m1(0)
                if a:
                    project2(ga, 1)
                    attn2_lo(ga, 3)
                if first:
                    conv_m1(1)
                if b:
                    turn1_lo(gb, 2)
                if a:
                    residual2(ga, 0)
                if b:
                    turn1_lo(gb, 3)
                if first:
                    conv_m1(2)
                    conv_m1(3)
                    conv_v1()
                if a:
                    project2(ga, 2)
                    if not b:
                        residual2(ga, 1)
                    project2(ga, 3)
                if b:
                    query1_lo(gb, 0)
                if a and b:
                    residual2(ga, 1)
                if b:
                    query1_lo(gb, 1)
                if first:
                    conv_next()
                if a:
                    residual2(ga, 2)
                if b:
                    query1_lo(gb, 2)
                if first:
                    conv_next()
                if a:
                    turn_lo(3, ga, 0)
                    residual2(ga, 3)
                if b:
                    query1_lo(gb, 3)
                if a:
                    turn_lo(3, ga, 1)
                if b:
                    value1_lo(gb, 0)
                if first:
                    conv_next()
                if a:
                    turn_lo(3, ga, 2)
                if b:
                    relation1(gb)
                if a:
                    turn_lo(3, ga, 3)
                if b:
                    relation1_lo(gb)
                    value1_lo(gb, 1)
                    ssq1(gb)
                if first:
                    conv_next()
                if a:
                    query_lo(3, ga, 0)
                if b:
                    value1_lo(gb, 2)
                if first:
                    conv_next()
                if a:
                    query_lo(3, ga, 1)
                if b:
                    value1_lo(gb, 3)
                for t in range(2, 4):
                    if a:
                        query_lo(3, ga, t)
                    if b:
                        residual1(gb, t - 2)
                for t in range(2):
                    if a:
                        key_lo(3, ga, t)
                    if b:
                        residual1(gb, t + 2)
                if a:
                    key_lo(3, ga, 2)
                    key_lo(3, ga, 3)
                    value_lo(3, ga, 0)
                    for t in range(2):
                        scores(3, ga, t)
                        softmax_max(3, ga, t)
                    softmax_sum(3, ga, 0)
                    value_lo(3, ga, 1)
                if b:
                    turn_lo(2, gb, 0)
                if a:
                    scores(3, ga, 2)
                    softmax_max(3, ga, 2)
                    softmax_sum(3, ga, 1)
                    value_lo(3, ga, 2)
                if b:
                    turn_lo(2, gb, 1)
                if a:
                    scores(3, ga, 3)
                    softmax_max(3, ga, 3)
                    softmax_sum(3, ga, 2)
                    value_lo(3, ga, 3)
                if b:
                    turn_lo(2, gb, 2)
                    turn_lo(2, gb, 3)
                if a:
                    softmax_sum(3, ga, 3)
                    weights_lo(3, ga, 0)
                    weights_lo(3, ga, 1)
                if first:
                    set_up_done()

            body(0, None, None)
            body(1, 0, None)
            with dve.Fori(2, GROUPS) as i:
                body(i, i - 1, i - 2)
            body(None, GROUPS - 1, GROUPS - 2)
            body(None, None, GROUPS - 1)

        @block.gpsimd
        def _(pool):
            pool.memset(adj_bd[:, :], 0.0).then_inc(const_ready, 1)
            pool.memset(neg_half[:, :], -0.5).then_inc(zero_ready, 1)
            pool.memset(ident[:, :], 0.0).then_inc(zero_ready, 1)
            pool.memset(ones[:, :], 1.0).then_inc(zero_ready, 1)
            pool.wait_ge(zero_ready, 3)
            pool.affine_select(out=ident[:, :], in_=ident[:, :], compare_op=ALU.not_equal, fill=1.0, base=0,
                               pattern=[[-1, P]], channel_multiplier=1).then_inc(ident_ready, 1)
            pool.wait_ge(setup_v, 4)
            pool.tensor_tensor(deg[:, 3:4], deg[:, 1:2], neg_half[:, :], ALU.pow).then_inc(setup_p, 1)

            def biases_here():
                pool.wait_ge(bias0_in, 16)

            def clear_blocks():
                for blocks in (q_hi, q_lo, pt_hi, pt_lo):
                    zero = pool.memset(blocks[:, :, :, :], 0.0)
                zero.then_inc(blocks_zero, 1)
                pool.wait_ge(small_in, 16 * 4)

            def root(L, g, t, bias=True):
                pool.wait_ge(mv_ready[L], 4 * g + t + 1)
                pool.sem_inc(passed_p, 1)
                pool.tensor_scalar(var_eps[:, L, t:t + 1], mean_var[:, L, t, 1:2], LN_EPS, None, ALU.add)\
                    .then_inc(ve_ready[L], 1)
                pool.wait_ge(ve_ready[L], 4 * g + t + 1)
                pool.tensor_tensor(rstd[:, L, t:t + 1], var_eps[:, L, t:t + 1], neg_half[:, :], ALU.pow)\
                    .then_inc(rstd_ready[L], 1)
                if bias:
                    pool.wait_ge(rstd_ready[L], 4 * g + t + 1)
                    pool.sem_inc(passed_p, 1)
                    pool.tensor_scalar(nbias[:, L, t:t + 1], rstd[:, L, t:t + 1], mean_var[:, L, t, 0:1], -1.0,
                                       ALU.mult, ALU.mult).then_inc(nbias_ready[L], 1)

            def add_rows(dst, a, b, sem_):
                pool.tensor_tensor(dst, a, b, ALU.add).then_inc(sem_, 1)

            def softmax_shift(L, g, t):
                pool.wait_ge(max_ready[L], 4 * g + t + 1)
                heads = work[:, t, :].rearrange("p (h k) -> p h k", h=H)
                pool.tensor_tensor(heads, heads, row_max[:, t, :].unsqueeze(2).broadcast_to((P, H, N)),
                                   ALU.subtract).then_inc(sub_ready[L], 1)

            def normalise(L, g, t):
                pool.wait_ge(inv_ready[L], 4 * g + t + 1)
                heads = work[:, t, :].rearrange("p (h k) -> p h k", h=H)
                pool.tensor_tensor(heads, heads, row_inv[:, t, :].unsqueeze(2).broadcast_to((P, H, N)),
                                   ALU.mult).then_inc(prob_ready, 1)

            def bias_rows0(g, t):
                pool.wait_ge(h_ready[0], 4 * g + t + 1)
                add_rows(x_in[:, t, :], x_in[:, t, :], bias0[:, :], xb0_ready)

            def beta_rows2(g, t):
                pool.wait_ge(b_lo, NB * g + J_OUT1 + t + 1)
                if counts(16 * g):
                    pool.wait_ge(y_stored[t], 16 * g)
                if is_group(g, 0):
                    pool.wait_ge(conv_lo, CONVERSIONS)
                add_rows(x_late[:, t, :], x_mid[:, t, :], beta[:, :], xbeta_ready)

            def output_rows2(g, t):
                pool.wait_ge(p_lo, NPJ * g + J_PR2 + t + 1)
                pool.wait_ge(xbeta_ready, 4 * g + t + 1)
                add_rows(x_late[:, t, :], x_late[:, t, :], work[:, t, :], xo_ready)

            def bias_rows3(g, t):
                pool.wait_ge(h_ready[3], 4 * g + t + 1)
                add_rows(x_late[:, t, :], x_late[:, t, :], biasv[:, :], xb3_ready)

            def norm1(g):
                pool.wait_ge(b_lo, NB * g + J_SSQ + 1)
                pool.tensor_tensor(rel_rn[:, :], rel_ssq[:, :], neg_half[:, :].broadcast_to((P, NT)), ALU.pow)\
                    .then_inc(rn_ready, 1)

            def body(gb, ga, gp):
                a, b, p = ga is not None, gb is not None, gp is not None
                first, second = is_group(gb, 0), is_group(ga, 0)
                if b:
                    for t in range(NT):
                        root(0, gb, t)
                if first:
                    biases_here()
                if b:
                    for t in range(NT):
                        bias_rows0(gb, t)
                if a:
                    for t in range(NT):
                        beta_rows2(ga, t)
                if b:
                    root(1, gb, 0)
                if a:
                    softmax_shift(2, ga, 0)
                    softmax_shift(2, ga, 1)
                    normalise(2, ga, 0)
                if b:
                    root(1, gb, 1)
                if a:
                    for t in range(2, 4):
                        softmax_shift(2, ga, t)
                        normalise(2, ga, t - 1)
                    normalise(2, ga, 3)
                if b:
                    root(1, gb, 2)
                    root(1, gb, 3)
                if first:
                    clear_blocks()
                if a:
                    for t in range(2):
                        output_rows2(ga, t)
                        root(4, ga, t, bias=False)
                    root(3, ga, 0)
                    for t in range(2, 4):
                        output_rows2(ga, t)
                        root(4, ga, t, bias=False)
                        if not b:
                            root(3, ga, t - 1)
                    for t in range(1 if b else 3, 4):
                        root(3, ga, t)
                if b:
                    norm1(gb)
                if a:
                    for t in range(NT):
                        bias_rows3(ga, t)
                if b:
                    for t in range(NT):
                        root(2, gb, t)
                if a:
                    softmax_shift(3, ga, 0)
                    for t in range(1, 4):
                        softmax_shift(3, ga, t)
                        normalise(3, ga, t - 1)
                    normalise(3, ga, 3)

            body(0, None, None)
            body(1, 0, None)
            with pool.Fori(2, GROUPS) as i:
                body(i, i - 1, i - 2)
            body(None, GROUPS - 1, GROUPS - 2)
            body(None, None, GROUPS - 1)


_INS = ['x', 'adj', 'L0_gnn_weight', 'L0_gnn_bias', 'L1_gnn_Wq', 'L1_gnn_Wk', 'L1_gnn_Wv', 'L2_gnn_w_qkv',
        'L2_gnn_w_proj', 'L2_gnn_b_proj', 'L2_gnn_ln_gamma', 'L2_gnn_ln_beta', 'L3_gnn_Wq', 'L3_gnn_bq',
        'L3_gnn_Wk', 'L3_gnn_bk', 'L3_gnn_Wv', 'L3_gnn_bv']
_OUTS = [((128, 64, 512), 'float32')]


def kernel(**inputs):
    import numpy as _np
    import concourse.bacc as _bacc
    from concourse import mybir as _mybir
    from concourse.bass_utils import run_bass_kernel_spmd as _run

    nc = _bacc.Bacc("TRN2", target_bir_lowering=False, num_devices=1)
    arrays, args = {}, []
    for name in _INS:
        a = _np.ascontiguousarray(inputs[name])
        arrays[f"in_{name}_dram"] = a
        args.append(nc.dram_tensor(f"in_{name}_dram", a.shape, _mybir.dt.from_np(a.dtype), kind="ExternalInput").ap())
    for i, (shape, dtype) in enumerate(_OUTS):
        dt = _mybir.dt.from_np(_np.dtype(dtype))
        args.append(nc.dram_tensor(f"out_{i}_dram", shape, dt, kind="ExternalOutput").ap())
    gnn_kernel(nc, *args)
    r = _run(nc, [arrays], core_ids=[0])
    got = tuple(r.results[0][f"out_{i}_dram"] for i in range(len(_OUTS)))
    return got[0]
```
